# Optimizing a Trainium2 kernel written in Bass

```python
import numpy as np
import jax
import jax.numpy as jnp

def _softmax(x, axis=-1):
    return jax.nn.softmax(x, axis=axis)

def _gelu(x):
    return jax.nn.gelu(x, approximate=True)

def _silu(x):
    return jax.nn.silu(x)

def _sigmoid(x):
    return jax.nn.sigmoid(x)

def _layernorm(x, axis=-1, eps=1e-05):
    m = jnp.mean(x, axis=axis, keepdims=True)
    v = jnp.var(x, axis=axis, keepdims=True)
    return (x - m) / jnp.sqrt(v + eps)

def _scatter_add(tgt, idx, src, axis=0):
    return tgt.at[idx].add(src)

def _segment_sum(src, seg, n):
    return jax.ops.segment_sum(src, seg, n)
kernel_name = 'mk_adaln_attn_ffn_d1_seqx_r8_466056'

def setup_inputs(seed: int=0):
    np.random.seed(seed)
    _w = jnp.asarray

    def _rec_inputs():
        import jax
        import jax.numpy as jnp
        _rk = jax.random.key(seed)
        x = -0.0003929 + 0.9999 * jax.random.normal(jax.random.fold_in(_rk, 1), (16, 128, 128), jnp.float32)
        _lenS = 128 - jax.random.randint(jax.random.fold_in(_rk, 7), (16,), 0, max(1, 128 // 4) + 1, jnp.int32)
        _lenS2 = 128 - jax.random.randint(jax.random.fold_in(_rk, 8), (16,), 0, max(1, 128 // 4) + 1, jnp.int32)
        cond_1024 = 0.00513981 + 1.0024 * jax.random.normal(jax.random.fold_in(_rk, 11), (16, 128), jnp.float32)
        return (x, cond_1024)
    x, cond_1024 = _rec_inputs()

    def _L0_cond_setup():
        import jax, jax.numpy as jnp
        import numpy as np
        D = 128
        H = 128
        key = jax.random.key(seed)
        k1, k2, k3, k4 = jax.random.split(key, 4)
        x = jax.random.normal(k1, (32, 64, D), dtype=jnp.float32)
        h0 = jax.random.normal(k2, (32, H), dtype=jnp.float32)
        Wx = jax.random.normal(k3, (D, 4 * H), dtype=jnp.float32) / jnp.sqrt(float(D))
        Wh = jax.random.normal(k4, (H, 4 * H), dtype=jnp.float32) / jnp.sqrt(float(H))
        b = jnp.zeros((4 * H,), dtype=jnp.float32)
        return {'x': x, 'h0': h0, 'Wx': Wx, 'Wh': Wh, 'b': b}
    _L0_cond_all = _L0_cond_setup()
    _L0_cond_in = {k: v for k, v in _L0_cond_all.items() if k in ('Wx', 'Wh', 'b')}
    del _L0_cond_all

    def _L0_attn_setup():
        import jax, jax.numpy as jnp
        import numpy as np
        import math
        IN_DIM = 128
        LATENT_DIM = 32
        OUT_DIM = 128

        def _kaiming(key, fan_out, fan_in):
            std = math.sqrt(2.0 / fan_in)
            return jax.random.normal(key, (fan_out, fan_in), dtype=jnp.float32) * std
        key = jax.random.key(seed)
        kx, kt, kp, kg = jax.random.split(key, 4)
        x = jax.random.normal(kx, (8, 512, IN_DIM), dtype=jnp.float32)
        W_theta = _kaiming(kt, LATENT_DIM, IN_DIM)
        W_phi = _kaiming(kp, LATENT_DIM, IN_DIM)
        W_g = _kaiming(kg, OUT_DIM, IN_DIM)
        return {'x': x, 'W_theta': W_theta, 'W_phi': W_phi, 'W_g': W_g}
    _L0_attn_all = _L0_attn_setup()
    _L0_attn_in = {k: v for k, v in _L0_attn_all.items() if k in ('W_theta', 'W_phi', 'W_g')}
    del _L0_attn_all

    def _L0_cond2_setup():
        import jax, jax.numpy as jnp
        import numpy as np
        import math
        N, T, D, H = (64, 64, 128, 128)
        key = jax.random.key(seed)
        k1, k2, k3, k4 = jax.random.split(key, 4)
        x = jax.random.normal(k1, (N, T, D), dtype=jnp.float32)
        h0 = jax.random.normal(k2, (N, H), dtype=jnp.float32)
        Wx = jax.random.normal(k3, (D, 4 * H), dtype=jnp.float32) / math.sqrt(D)
        Wh = jax.random.normal(k4, (H, 4 * H), dtype=jnp.float32) / math.sqrt(H)
        b = jnp.zeros((4 * H,), dtype=jnp.float32)
        return {'x': x, 'h0': h0, 'Wx': Wx, 'Wh': Wh, 'b': b}
    _L0_cond2_all = _L0_cond2_setup()
    _L0_cond2_in = {k: v for k, v in _L0_cond2_all.items() if k in ('Wx', 'Wh', 'b')}
    del _L0_cond2_all

    def _L0_ffn_setup():
        import jax, jax.numpy as jnp
        import numpy as np
        HIDDEN = 128
        INTER = 512
        key = jax.random.key(seed)
        k1, k2, k3, k4, k5 = jax.random.split(key, 5)
        hidden_states = jax.random.normal(k1, (4, 256, HIDDEN), dtype=jnp.float32)
        W1 = jax.random.normal(k2, (HIDDEN, INTER), dtype=jnp.float32) * (1.0 / np.sqrt(HIDDEN))
        b1 = jax.random.normal(k3, (INTER,), dtype=jnp.float32) * 0.02
        W2 = jax.random.normal(k4, (INTER, HIDDEN), dtype=jnp.float32) * (1.0 / np.sqrt(INTER))
        b2 = jax.random.normal(k5, (HIDDEN,), dtype=jnp.float32) * 0.02
        return {'hidden_states': hidden_states, 'W1': W1, 'b1': b1, 'W2': W2, 'b2': b2}
    _L0_ffn_all = _L0_ffn_setup()
    _L0_ffn_in = {k: v for k, v in _L0_ffn_all.items() if k in ('W1', 'b1', 'W2', 'b2')}
    del _L0_ffn_all
    return {'x': x, 'cond_1024': cond_1024, 'L0_cond_Wx': _L0_cond_in['Wx'], 'L0_cond_Wh': _L0_cond_in['Wh'], 'L0_cond_b': _L0_cond_in['b'], 'L0_attn_W_theta': _L0_attn_in['W_theta'], 'L0_attn_W_phi': _L0_attn_in['W_phi'], 'L0_attn_W_g': _L0_attn_in['W_g'], 'L0_cond2_Wx': _L0_cond2_in['Wx'], 'L0_cond2_Wh': _L0_cond2_in['Wh'], 'L0_cond2_b': _L0_cond2_in['b'], 'L0_ffn_W1': _L0_ffn_in['W1'], 'L0_ffn_b1': _L0_ffn_in['b1'], 'L0_ffn_W2': _L0_ffn_in['W2'], 'L0_ffn_b2': _L0_ffn_in['b2']}

def reference(x, cond_1024, L0_cond_Wx, L0_cond_Wh, L0_cond_b, L0_attn_W_theta, L0_attn_W_phi, L0_attn_W_g, L0_cond2_Wx, L0_cond2_Wh, L0_cond2_b, L0_ffn_W1, L0_ffn_b1, L0_ffn_W2, L0_ffn_b2):
    import jax
    import jax.numpy as jnp

    def _L0_cond_ref(x, h0, Wx, Wh, b):
        import jax, jax.numpy as jnp
        import numpy as np
        D = 128
        H = 128
        Hdim = h0.shape[1]
        x_proj = jnp.einsum('ntd,df->ntf', x, Wx) + b

        def step(carry, xp_t):
            prev_h, prev_c = carry
            h_bar = xp_t + prev_h @ Wh
            i = jax.nn.sigmoid(h_bar[:, 0:Hdim])
            f = jax.nn.sigmoid(h_bar[:, Hdim:2 * Hdim])
            o = jax.nn.sigmoid(h_bar[:, 2 * Hdim:3 * Hdim])
            g = jnp.tanh(h_bar[:, 3 * Hdim:4 * Hdim])
            next_c = f * prev_c + i * g
            next_h = o * jnp.tanh(next_c)
            return ((next_h, next_c), next_h)
        c0 = jnp.zeros_like(h0)
        xs = jnp.swapaxes(x_proj, 0, 1)
        _, hs = jax.lax.scan(step, (h0, c0), xs)
        return jnp.swapaxes(hs, 0, 1)

    def _L0_attn_ref(x, W_theta, W_phi, W_g):
        import jax, jax.numpy as jnp
        import numpy as np
        import math
        IN_DIM = 128
        LATENT_DIM = 32
        OUT_DIM = 128

        def _kaiming(key, fan_out, fan_in):
            std = math.sqrt(2.0 / fan_in)
            return jax.random.normal(key, (fan_out, fan_in), dtype=jnp.float32) * std
        theta_x = jnp.einsum('bnf,lf->bnl', x, W_theta)
        phi_x = jnp.einsum('bnf,lf->bnl', x, W_phi)
        fun_g_x = jnp.einsum('bnf,of->bno', x, W_g)
        scale = 1.0 / math.sqrt(IN_DIM)
        att = jnp.einsum('bnl,bml->bnm', theta_x, phi_x) * scale
        return jnp.einsum('bnm,bmo->bno', att, fun_g_x)

    def _L0_cond2_ref(x, h0, Wx, Wh, b):
        import jax, jax.numpy as jnp
        import numpy as np
        import math
        N, T, D, H = (64, 64, 128, 128)
        Hdim = h0.shape[1]
        c0 = jnp.zeros_like(h0)
        xW = jnp.einsum('ntd,dk->tnk', x, Wx) + b

        def step(carry, xw_t):
            prev_h, prev_c = carry
            a = xw_t + prev_h @ Wh
            i = jax.nn.sigmoid(a[:, :Hdim])
            f = jax.nn.sigmoid(a[:, Hdim:2 * Hdim])
            o = jax.nn.sigmoid(a[:, 2 * Hdim:3 * Hdim])
            g = jnp.tanh(a[:, 3 * Hdim:])
            next_c = f * prev_c + i * g
            next_h = o * jnp.tanh(next_c)
            return ((next_h, next_c), next_h)
        _, hs = jax.lax.scan(step, (h0, c0), xW)
        return jnp.transpose(hs, (1, 0, 2))

    def _L0_ffn_ref(hidden_states, W1, b1, W2, b2):
        import jax, jax.numpy as jnp
        import numpy as np
        HIDDEN = 128
        INTER = 512
        h = jax.nn.relu(jnp.einsum('bsh,hi->bsi', hidden_states, W1) + b1)
        return jnp.einsum('bsi,ih->bsh', h, W2) + b2
    x = x + _L0_attn_ref(_L0_cond_ref(x, cond_1024, L0_cond_Wx, L0_cond_Wh, L0_cond_b), L0_attn_W_theta, L0_attn_W_phi, L0_attn_W_g)
    x = x + _L0_ffn_ref(_L0_cond2_ref(x, cond_1024, L0_cond2_Wx, L0_cond2_Wh, L0_cond2_b), L0_ffn_W1, L0_ffn_b1, L0_ffn_W2, L0_ffn_b2)
    return x

_drawn_inputs = setup_inputs


def setup_inputs(seed=0):
    import zlib

    import numpy as np

    out = dict(_drawn_inputs(seed))
    spreads = {'L0_cond_b': (0.0, 0.1), 'L0_cond2_b': (0.0, 0.294)}
    factors = {'L0_ffn_b1': 4.233, 'L0_ffn_b2': 2.885}
    for name, (base, spread) in spreads.items():
        noise = np.random.default_rng([zlib.crc32(name.encode()), seed]).standard_normal(out[name].shape)
        drawn = base * np.exp(spread * noise) if base else spread * noise
        out[name] = jnp.asarray(drawn.astype(out[name].dtype))
    for name, factor in factors.items():
        out[name] = (out[name] * factor).astype(out[name].dtype)
    return out
```

```python
import math
from contextlib import ExitStack

import concourse.bass as bass
from concourse import mybir


def build(nc, x, cond, l1_wx, l1_wh, l1_b, w_theta, w_phi, w_g,
          l2_wx, l2_wh, l2_b, f_w1, f_b1, f_w2, f_b2, out):
    f32 = mybir.dt.float32
    bf16 = mybir.dt.bfloat16
    f16 = mybir.dt.float16
    ALU = mybir.AluOpType
    ACT = mybir.ActivationFunctionType

    NB, T, D = x.shape
    H = D
    LAT = w_theta.shape[0]
    P = 128
    CH = P // NB
    NCH = T // CH
    ITER = NCH // 2
    STEPS = 2 * CH
    NJ = f_w1.shape[1] // P
    WARM1 = [1, 1, 1, 1, 3, 3, 3, 3]
    WARM2 = [1, 1, 0, 1, 1, 1, 1, 1]
    GI, GF, GO, GG = range(4)
    FIG = [GG, GF, GI]
    HS = 2.0 ** 14
    H_UNIT = 2.0 * HS
    SC_OUT = 1.0 / math.sqrt(D)

    ctx = ExitStack()
    with ctx:
        def sb(name, shape, dt=f32):
            return ctx.enter_context(nc.sbuf_tensor(name, shape, dt))

        def ps(name):
            return ctx.enter_context(nc.psum_tensor(name, [P, 512], f32))

        def sem(name):
            return ctx.enter_context(nc.semaphore(name))

        x_rows = sb("x_rows", [P, NCH, D])
        xT = sb("xT", [P, NCH + 1, P])
        x2T = sb("x2T", [P, NCH + 1, P])
        ident = sb("ident", [P, P])
        ones = sb("ones", [P, P])
        wx = [sb(f"wx{n}", [P, 4 * H]) for n in (1, 2)]
        wh = [sb(f"wh{n}", [P, 4 * H]) for n in (1, 2)]
        bias = [sb(f"bias{n}", [P, 4 * H]) for n in (1, 2)]
        cond_rows = sb("cond_rows", [NB, H])
        h0 = sb("h0", [P, NB])
        wh_parts = [sb(f"wh_parts{n}", [P, 3, 4 * H], bf16) for n in (1, 2)]
        wh_rest = [sb(f"wh_rest{n}", [P, 4 * H]) for n in (1, 2)]
        wtp = sb("wtp", [P, 2, D])
        wg_rows = sb("wg_rows", [P, D])
        proj = sb("proj", [P, 2, D])
        w1 = sb("w1", [P, NJ * P])
        w2 = sb("w2", [P, NJ, D])
        b1 = sb("b1", [P, NJ])
        b2 = sb("b2", [P, D])
        gates = sb("gates", [P, 2, 4 * NB])
        ogate = sb("ogate", [P, NB])
        ogate1 = sb("ogate1", [P, NB])
        h_hi = sb("h_hi", [P, STEPS, NB], f16)
        h_lo = sb("h_lo", [P, STEPS, NB], f16)
        prods = sb("prods", [P, 2 * NB])
        warm = sb("warm", [P, 1])
        warm_w = sb("warm_w", [P, P], bf16)
        warm_x = sb("warm_x", [P, 512], bf16)
        ring = sb("ring", [P, STEPS, NB])
        hist = sb("hist", [P, NCH, P])
        hpg = sb("hpg", [P, 2, 2, 2 * D])
        pb = sb("pb", [P, NB, D])
        xin = sb("xin", [P, 2, P])
        xres = sb("xres", [P, 2, P])
        relu = sb("relu", [P, NJ, P])
        y_sb = sb("y_sb", [P, 2, D])

        fig = [ps("fig0"), ps("fig1")]
        ob = [ps("ob0"), ps("ob1")]
        cell = ps("cell")
        bankU, bankV, bankY = ps("bankU"), ps("bankV"), ps("bankY")
        c_psum, tanhc = cell[:, 0:NB], cell[:, NB:2 * NB]

        s_id = sem("s_id")
        s_w1l = sem("s_w1l")
        s_w2l = sem("s_w2l")
        s_x0 = sem("s_x0")
        s_xr = sem("s_xr")
        s_setA = sem("s_setA")
        s_setB = sem("s_setB")
        s_scale = sem("s_scale")
        s_tr = sem("s_tr")
        quad_done = sem("quad_done")
        h0_done = sem("h0_done")
        proj_done = sem("proj_done")
        fig_ready = [sem("fig_ready1"), sem("fig_ready2")]
        o_ready = [sem("o_ready1"), sem("o_ready2")]
        gates_done = [sem("gates_done1"), sem("gates_done2")]
        tanh_done = [sem("tanh_done1"), sem("tanh_done2")]
        prod_done = [sem("prod_done1"), sem("prod_done2")]
        c_ready = [sem("c_ready1"), sem("c_ready2")]
        h_ready = [sem("h_ready1"), sem("h_ready2")]
        hi_ready = [sem("hi_ready1"), sem("hi_ready2")]
        lo_ready = [sem("lo_ready1"), sem("lo_ready2")]
        s_part = [sem("s_part1"), sem("s_part2")]
        hist_saved = [sem("hist_saved0"), sem("hist_saved1")]
        a_mm1 = sem("a_mm1")
        a_cp1 = sem("a_cp1")
        a_mm2 = sem("a_mm2")
        a_cp2 = sem("a_cp2")
        a_mm3 = sem("a_mm3")
        x2_done = sem("x2_done")
        xin_loaded = [sem("xin_loaded0"), sem("xin_loaded1")]
        xres_loaded = [sem("xres_loaded0"), sem("xres_loaded1")]
        xp_done = sem("xp_done")
        u_ready = sem("u_ready")
        relu_done = sem("relu_done")
        y_ready = sem("y_ready")
        y_copied = sem("y_copied")
        y_stored = [sem("y_stored0"), sem("y_stored1")]

        block = ctx.enter_context(nc.Block())

        def gate_cols(g):
            return slice(g * H, (g + 1) * H)

        x_tb = x.rearrange("b (c t) d -> t b c d", t=CH)
        out_tb = out.rearrange("b (c t) d -> c t b d", t=CH)

        def split_wh(eng, e, layer):
            done, w, parts, rest = s_part[layer], wh[layer], wh_parts[layer], wh_rest[layer]
            for k in range(3):
                src = w if k == 0 else rest
                e.tensor_copy(parts[:, k, :], src[:]).then_inc(done, 1)
                eng.wait_ge(done, 2 * k + 1)
                if k < 2:
                    e.tensor_tensor(out=rest[:], in0=src[:], in1=parts[:, k, :], op=ALU.subtract).then_inc(done, 1)
                    eng.wait_ge(done, 2 * k + 2)

        def start_h(layer):
            nc.vector.memset(h_hi[:, STEPS - 1, :], 0.0).then_inc(hi_ready[layer], 1)
            nc.vector.memset(h_lo[:, STEPS - 1, :], 0.0).then_inc(lo_ready[layer], 1)
            nc.vector.memset(gates[:, 0, 0:NB], 0.0)

        @block.sync
        def _(sp):
            sp.dma_start(cond_rows[:], cond).then_inc(s_x0, 16)
            for t in range(CH):
                sp.dma_start(x_rows[NB * t:NB * t + NB, :, :], x_tb[t]).then_inc(s_xr, 16)
            sp.sem_inc(hist_saved[0], 16)
            sp.sem_inc(hist_saved[1], 16)
            with sp.Fori(0, ITER) as i:
                for half in range(2):
                    sp.wait_ge(h_ready[0], i * STEPS + CH * (half + 1))
                    sp.dma_start(hist[:, bass.ds(i * 2 + half, 1), :],
                                 ring[:, CH * half:CH * half + CH, :].rearrange("p t b -> p (t b)").unsqueeze(1)
                                 ).then_inc(hist_saved[half], 16)
            sp.wait_ge(x2_done, NB)
            sp.dma_start(xin[:, 0, :], x2T[:, 0, :]).then_inc(xin_loaded[0], 16)
            sp.wait_ge(s_setB, 2)
            sp.dma_start(xres[:, 1, :], x2T[:, NCH, :]).then_inc(xres_loaded[1], 16)
            sp.sem_inc(y_stored[0], 16)
            sp.sem_inc(y_stored[1], 32)

            def bring(i, half):
                c = i * 2 + half
                if not (isinstance(c, int) and c == 0):
                    sp.wait_ge(y_ready, c)
                sp.dma_start(xres[:, half:half + 1, :], x2T[:, bass.ds(c, 1), :]).then_inc(xres_loaded[half], 16)
                if not (isinstance(c, int) and c == 0):
                    sp.wait_ge(xp_done, c)
                sp.dma_start(xin[:, 1 - half:2 - half, :], x2T[:, bass.ds(c + 1, 1), :]).then_inc(xin_loaded[1 - half], 16)

            def store(c, slot, count):
                sp.wait_ge(y_copied, count + 1)
                sp.dma_start(out_tb[c], y_sb[:, slot, :]).then_inc(y_stored[slot], 16)

            bring(0, 0)
            bring(0, 1)
            store(0, 0, 2)
            with sp.Fori(1, ITER) as i:
                bring(i, 0)
                c1 = sp.snap(i * 2 - 1)
                sp.wait_ge(y_copied, c1 + 3)
                sp.dma_start(out_tb[bass.ds(c1, 1)].rearrange("o t b d -> (o t) b d"), y_sb[:, 1, :]).then_inc(y_stored[1], 16)
                bring(i, 1)
                c2 = sp.snap(i * 2)
                sp.wait_ge(y_copied, c2 + 3)
                sp.dma_start(out_tb[bass.ds(c2, 1)].rearrange("o t b d -> (o t) b d"), y_sb[:, 0, :]).then_inc(y_stored[0], 16)
            store(NCH - 1, 1, NCH + 1)
            for slot in range(2):
                sp.wait_ge(y_stored[slot], 16 * (NCH // 2 + 1 + slot))

        SETB = 2 + 4 + 1

        @block.gpsimd
        def _(pool):
            nc.gpsimd.memset(ident[:], 0.0).then_inc(s_id, 1)
            pool.wait_ge(s_id, 1)
            nc.gpsimd.affine_select(out=ident[:], in_=ident[:], compare_op=ALU.not_equal, fill=1.0, base=0,
                                    pattern=[[-1, P]], channel_multiplier=1).then_inc(s_id, 1)
            nc.gpsimd.memset(bias[1][:], 0.0).then_inc(s_setA, 1)
            nc.gpsimd.memset(wtp[:], 0.0).then_inc(s_setA, 1)
            pool.wait_ge(s_setA, 2)
            pool.dma_start(bias[1][0:1, :], l2_b.unsqueeze(0)).then_inc(s_w2l, 16)
            pool.dma_start(wtp[0:LAT, 0, :], w_theta).then_inc(s_w2l, 16)
            pool.dma_start(wtp[0:LAT, 1, :], w_phi).then_inc(s_w2l, 16)
            pool.dma_start(wg_rows[:], w_g).then_inc(s_w2l, 16)
            pool.dma_start(wx[1][:], l2_wx).then_inc(s_w2l, 16)
            pool.dma_start(wh[1][:], l2_wh).then_inc(s_w2l, 16)
            pool.dma_start(w1[:], f_w1).then_inc(s_w2l, 16)
            pool.dma_start(w2[:], f_w2.rearrange("(j p) d -> p j d", p=P)).then_inc(s_w2l, 16)
            pool.dma_start(b1[:], f_b1.rearrange("(j p) -> p j", p=P), allow_slow_non_contiguous=True).then_inc(s_w2l, 16)
            pool.dma_start(b2[:], f_b2.unsqueeze(0).broadcast_to([P, D])).then_inc(s_w2l, 16)
            nc.gpsimd.memset(xT[:, NCH, :], 0.0).then_inc(s_setB, 1)
            nc.gpsimd.memset(x2T[:, NCH, :], 0.0).then_inc(s_setB, 1)
            pool.wait_ge(s_w2l, 160)
            for n, src in enumerate((wx[1], wh[1], bias[1])):
                by = 1.0 / H_UNIT if n == 1 else 1.0
                nc.gpsimd.tensor_scalar(src[:, 0:3 * H], src[:, 0:3 * H], 0.5 * by, None, ALU.mult).then_inc(s_setB, 1)
                if n == 1:
                    nc.gpsimd.tensor_scalar(src[:, 3 * H:], src[:, 3 * H:], by, None, ALU.mult).then_inc(s_setB, 1)
            nc.gpsimd.tensor_scalar(w1[:], w1[:], 1.0 / H_UNIT, None, ALU.mult).then_inc(s_setB, 1)
            pool.wait_ge(s_setB, SETB)
            split_wh(pool, nc.gpsimd, 1)

        @block.tensor
        def _(pe):
            def project_gate(layer, p, g, rhs):
                if g == GO:
                    dst = ob[p][:, 0:P]
                    first = True
                else:
                    k = FIG.index(g)
                    dst = fig[p][:, 0:3 * P].rearrange("p (t g b) -> p t g b", g=3, b=NB)[:, :, k, :]
                    first = k == 0
                r = rhs.rearrange("p (t b) -> p t b", b=NB) if g != GO else rhs
                o = ones[:, :].rearrange("p (t b) -> p t b", b=NB) if g != GO else ones[:, :]
                nc.tensor.matmul(dst, wx[layer][:, gate_cols(g)], r, start=first, stop=False, skip_group_check=True)
                return nc.tensor.matmul(dst, bias[layer][:, gate_cols(g)], o, start=False, stop=False,
                                        skip_group_check=True)

            def initial(layer):
                for g in FIG + [GO]:
                    dst = ob[0][:, 0:NB] if g == GO else fig[0][:, FIG.index(g) * NB:FIG.index(g) * NB + NB]
                    nc.tensor.matmul(dst, wh[layer][:, gate_cols(g)], h0[:], start=False, stop=True,
                                     skip_group_check=True)

            def keep_warm(bank, n):
                for _ in range(n):
                    nc.tensor.matmul(bank[:, :], warm_w[:], warm_x[:], start=True, stop=True)

            def step(layer, s, count):
                p, t = s // CH, s % CH
                def passes(h, gs):
                    for g in gs:
                        if g == GO:
                            dst = ob[p][:, NB * t:NB * t + NB]
                        else:
                            c0 = (3 * t + FIG.index(g)) * NB
                            dst = fig[p][:, c0:c0 + NB]
                        for part in range(3):
                            last = nc.tensor.matmul(dst, wh_parts[layer][:, part, gate_cols(g)],
                                                    h[:, (s - 1) % STEPS, :],
                                                    start=False, stop=True, skip_group_check=True)
                    return last

                pe.wait_ge(hi_ready[layer], count)
                passes(h_hi, FIG)
                pe.wait_ge(lo_ready[layer], count)
                passes(h_lo, FIG).then_inc(fig_ready[layer], 1)
                passes(h_hi, [GO])
                passes(h_lo, [GO]).then_inc(o_ready[layer], 1)

            pe.wait_ge(s_id, 2)
            pe.wait_ge(s_x0, 16)
            nc.tensor.transpose(bankY[:, 0:NB], cond_rows[:], ident[0:NB, 0:NB]).then_inc(s_tr, 1)
            pe.wait_ge(s_xr, 16 * CH)
            for q in range(NCH // 4):
                bank = (bankU, bankV)[q % 2]
                if q >= 2:
                    pe.wait_ge(quad_done, q - 1)
                for c in range(4):
                    last = nc.tensor.transpose(bank[:, c * P:c * P + P], x_rows[:, 4 * q + c, :], ident[:])
                last.then_inc(s_tr, 1)
            pe.wait_ge(quad_done, 1)
            pe.wait_ge(s_scale, 6)
            for g in FIG + [GO]:
                project_gate(0, 0, g, xT[:, 0, :])
            pe.wait_ge(h0_done, 1)
            initial(0)
            pe.wait_ge(quad_done, NCH // 4)
            pe.wait_ge(s_part[0], 5)
            pe.wait_ge(s_setB, 1)
            with pe.Fori(0, ITER) as i:
                for s in range(STEPS):
                    p, t = s // CH, s % CH
                    step(0, s, i * STEPS + (s + 1))
                    if t < 4:
                        g = (FIG + [GO])[t]
                        rhs = xT[:, bass.ds(i * 2 + (p + 1), 1), :].rearrange("p c n -> p (c n)")
                        project_gate(0, 1 - p, g, rhs)
                    else:
                        pass
                    keep_warm(bankV, WARM1[t])

            pe.wait_ge(s_w2l, 160)
            nc.tensor.matmul(bankU[:, 0:P], wtp[:, 1, :], wtp[:, 0, :], start=True, stop=True).then_inc(s_tr, 1)
            nc.tensor.transpose(bankV[:, 0:P], wg_rows[:], ident[:]).then_inc(s_tr, 1)
            pe.wait_ge(proj_done, 2)
            for half in range(2):
                pe.wait_ge(hist_saved[half], 16 * ITER + 16)
            hist_b = hist[:].rearrange("p c (t b) -> p b (c t)", b=NB)
            mm1 = [bankU, bankV]
            for pair in range(NB // 2):
                if pair >= 2:
                    pe.wait_ge(a_cp1, pair - 1)
                for k in range(2):
                    last = nc.tensor.matmul(mm1[pair % 2][:, 256 * k:256 * k + 256], hist_b[:, 2 * pair + k, :],
                                            proj[:].rearrange("p a n -> p (a n)"), start=True, stop=True)
                last.then_inc(a_mm1, 1)
                if pair >= 1:
                    q = pair - 1
                    pe.wait_ge(a_cp1, q + 1)
                    if q >= 2:
                        pe.wait_ge(a_cp2, q - 1)
                    for k in range(2):
                        last = nc.tensor.matmul((bankY, cell)[q % 2][:, P * k:P * k + P], hpg[:, q % 2, k, 0:D],
                                                hpg[:, q % 2, k, D:2 * D], start=True, stop=True)
                    last.then_inc(a_mm2, 1)
            q = NB // 2 - 1
            pe.wait_ge(a_cp1, q + 1)
            pe.wait_ge(a_cp2, q - 1)
            for k in range(2):
                last = nc.tensor.matmul((bankY, cell)[q % 2][:, P * k:P * k + P], hpg[:, q % 2, k, 0:D],
                                        hpg[:, q % 2, k, D:2 * D], start=True, stop=True)
            last.then_inc(a_mm2, 1)
            for b in range(NB):
                pe.wait_ge(a_cp2, b // 2 + 1)
                if b >= 2:
                    pe.wait_ge(x2_done, b - 1)
                nc.tensor.matmul((bankU, bankV)[b % 2][:, 0:P], pb[:, b, :], hist_b[:, b, :],
                                 start=True, stop=True).then_inc(a_mm3, 1)

            pe.wait_ge(s_setB, SETB)
            pe.wait_ge(s_part[1], 5)
            pe.wait_ge(xin_loaded[0], 16)
            for g in FIG + [GO]:
                last = project_gate(1, 0, g, xin[:, 0, :])
            last.then_inc(xp_done, 1)
            initial(1)

            def ffn_up(half, j):
                return nc.tensor.matmul(bankU[:, P * j:P * j + P],
                                        w1[:, j * P:j * P + P],
                                        ring[:, CH * half:CH * half + CH, :].rearrange("p t b -> p (t b)"),
                                        start=True, stop=True)

            def ffn_down(j):
                return nc.tensor.matmul(bankY[:, 0:D], relu[:, j, :], w2[:, j, :], start=False, stop=(j == NJ - 1))

            def residual(half):
                return nc.tensor.matmul(bankY[:, 0:D], xres[:, half, :], ident[:], start=True, stop=False)

            with pe.Fori(0, ITER) as i:
                for s in range(STEPS):
                    p, t = s // CH, s % CH
                    step(1, s, i * STEPS + (s + 1))
                    c = i * 2 + p
                    if t == 0:
                        for j in range(2):
                            ffn_up(1 - p, j)
                    if t == 1:
                        for j in range(2, 4):
                            last = ffn_up(1 - p, j)
                        last.then_inc(u_ready, 1)
                    if t == 2:
                        pe.wait_ge(xres_loaded[1 - p], i * 16 + 16)
                        pe.wait_ge(y_copied, c + 1)
                        residual(1 - p)
                    if t == 4:
                        pe.wait_ge(relu_done, c * 4 + 2)
                        ffn_down(0)
                        ffn_down(1)
                    if t == 5:
                        pe.wait_ge(relu_done, c * 4 + 4)
                        ffn_down(2)
                        ffn_down(3).then_inc(y_ready, 1)
                    if t == 2:
                        pe.wait_ge(xin_loaded[1 - p], i * 16 + 16 * (p + 1))
                    if t in (2, 3, 6, 7):
                        last = project_gate(1, 1 - p, {2: FIG[0], 3: FIG[1], 6: FIG[2], 7: GO}[t], xin[:, 1 - p, :])
                    if t == 7:
                        last.then_inc(xp_done, 1)
                    keep_warm(bankV, WARM2[t])
            pe.wait_ge(h_ready[1], T)
            for j in range(4):
                last = ffn_up(1, j)
            last.then_inc(u_ready, 1)
            pe.wait_ge(xres_loaded[1], 16 * (ITER + 1))
            pe.wait_ge(y_copied, NCH + 1)
            residual(1)
            for j in range(4):
                if j % 2 == 0:
                    pe.wait_ge(relu_done, 4 * NCH + 2 + j)
                last = ffn_down(j)
            last.then_inc(y_ready, 1)

        @block.scalar
        def _(act):
            act.dma_start(wx[0][:], l1_wx).then_inc(s_w1l, 16)
            act.dma_start(wh[0][:], l1_wh).then_inc(s_w1l, 16)
            act.wait_ge(s_scale, 1)
            act.dma_start(bias[0][0:1, :], l1_b.unsqueeze(0)).then_inc(s_w1l, 16)
            act.wait_ge(s_id, 2)
            nc.scalar.activation(warm[:], ident[:, 0:1], ACT.Tanh)
            act.wait_ge(s_tr, 1)
            nc.scalar.mul(h0[:], bankY[:, 0:NB], H_UNIT).then_inc(h0_done, 1)

            def step(layer, s, n):
                p, t = s // CH, s % CH
                n1 = n + 1
                act.wait_ge(fig_ready[layer], n1)
                nc.scalar.activation(gates[:, s % 2, NB:4 * NB], fig[p][:, 3 * NB * t:3 * NB * (t + 1)],
                                     ACT.Tanh).then_inc(gates_done[layer], 1)
                act.wait_ge(o_ready[layer], n1)
                nc.scalar.activation(ogate[:], ob[p][:, NB * t:NB * t + NB], ACT.Tanh).then_inc(tanh_done[layer], 1)
                act.wait_ge(tanh_done[layer], n * 3 + 1)
                nc.scalar.activation(ogate1[:], ogate[:], ACT.Identity, bias=HS, scale=HS).then_inc(tanh_done[layer], 1)
                act.wait_ge(c_ready[layer], n1)
                nc.scalar.activation(tanhc, c_psum, ACT.Tanh,
                                     scale=0.5).then_inc(tanh_done[layer], 1)

            with act.Fori(0, ITER) as i:
                for s in range(STEPS):
                    step(0, s, i * STEPS + s)
            act.wait_ge(s_tr, 2 + NCH // 4)
            nc.scalar.mul(proj[:, 0, :], bankU[:, 0:P], SC_OUT / H_UNIT ** 2).then_inc(proj_done, 1)
            act.wait_ge(s_tr, 3 + NCH // 4)
            nc.scalar.mul(proj[:, 1, :], bankV[:, 0:P], 1.0 / H_UNIT).then_inc(proj_done, 1)
            for pair in range(NB // 2):
                act.wait_ge(a_mm1, pair + 1)
                if pair >= 2:
                    act.wait_ge(a_mm2, pair - 1)
                nc.scalar.copy(hpg[:, pair % 2, :, :].rearrange("p a n -> p (a n)"),
                               (bankU, bankV)[pair % 2][:, :]).then_inc(a_cp1, 1)
            with act.Fori(0, ITER) as i:
                for s in range(STEPS):
                    step(1, s, i * STEPS + s)

        @block.vector
        def _(dve):
            nc.vector.memset(bias[0][:], 0.0).then_inc(s_scale, 1)
            nc.vector.memset(ones[:], 1.0).then_inc(s_scale, 1)
            nc.vector.memset(warm_w[:], 1.0)
            nc.vector.memset(warm_x[:], 1.0)
            dve.wait_ge(s_w1l, 48)
            for n, src in enumerate((wx[0], wh[0], bias[0])):
                by = 1.0 / H_UNIT if n == 1 else 1.0
                nc.vector.tensor_scalar(src[:, 0:3 * H], src[:, 0:3 * H], 0.5 * by, None, ALU.mult).then_inc(s_scale, 1)
                if n == 1:
                    nc.vector.tensor_scalar(src[:, 3 * H:], src[:, 3 * H:], by, None, ALU.mult).then_inc(s_scale, 1)
            dve.wait_ge(s_scale, 6)
            split_wh(dve, nc.vector, 0)
            start_h(0)
            for q in range(NCH // 4):
                dve.wait_ge(s_tr, 2 + q)
                nc.vector.tensor_copy(xT[:, 4 * q:4 * q + 4, :].rearrange("p c n -> p (c n)"),
                                      (bankU, bankV)[q % 2][:, :]).then_inc(quad_done, 1)

            def step(layer, s, n, extra_wait=None):
                p = s % 2
                n1 = n + 1
                dve.wait_ge(gates_done[layer], n1)
                nc.vector.scalar_tensor_tensor(out=prods[:], in0=gates[:, p, 2 * NB:4 * NB], scalar=1.0,
                                               in1=gates[:, p, 0:2 * NB], op0=ALU.add,
                                               op1=ALU.mult).then_inc(prod_done[layer], 1)
                dve.wait_ge(prod_done[layer], n1)
                nc.vector.scalar_tensor_tensor(out=c_psum, in0=prods[:, 0:NB], scalar=0.5,
                                               in1=prods[:, NB:2 * NB], op0=ALU.mult,
                                               op1=ALU.add).then_inc(c_ready[layer], 1)
                nc.vector.scalar_tensor_tensor(out=gates[:, 1 - p, 0:NB], in0=prods[:, 0:NB], scalar=0.5,
                                               in1=prods[:, NB:2 * NB], op0=ALU.mult,
                                               op1=ALU.add)
                if extra_wait:
                    dve.wait_ge(*extra_wait)
                dve.wait_ge(tanh_done[layer], n * 3 + 3)
                nc.vector.tensor_tensor(out=h_hi[:, s, :], in0=ogate1[:], in1=tanhc,
                                        op=ALU.mult).then_inc(hi_ready[layer], 1)
                nc.vector.tensor_tensor(out=ring[:, s, :], in0=ogate1[:], in1=tanhc,
                                        op=ALU.mult).then_inc(h_ready[layer], 1)
                dve.wait_ge(h_ready[layer], n1)
                nc.vector.tensor_tensor(out=h_lo[:, s, :], in0=ring[:, s, :], in1=h_hi[:, s, :],
                                        op=ALU.subtract).then_inc(lo_ready[layer], 1)

            with dve.Fori(0, ITER) as i:
                for s in range(STEPS):
                    step(0, s, i * STEPS + s, (hist_saved[s // CH], i * 16 + 16) if s % CH == 0 else None)
            dve.wait_ge(hist_saved[1], 16 * ITER + 16)
            dve.wait_ge(lo_ready[0], T + 1)
            start_h(1)
            for pair in range(NB // 2):
                dve.wait_ge(a_mm2, pair + 1)
                nc.vector.tensor_copy(pb[:, 2 * pair:2 * pair + 2, :].rearrange("p a n -> p (a n)"),
                                      (bankY, cell)[pair % 2][:, 0:2 * P]).then_inc(a_cp2, 1)
            xb = xT[:, 0:NCH, :].rearrange("p c (t b) -> p b (c t)", b=NB)
            x2b = x2T[:, 0:NCH, :].rearrange("p c (t b) -> p b (c t)", b=NB)
            for b in range(NB):
                dve.wait_ge(a_mm3, b + 1)
                nc.vector.tensor_tensor(out=x2b[:, b, :], in0=(bankU, bankV)[b % 2][:, 0:P], in1=xb[:, b, :],
                                        op=ALU.add).then_inc(x2_done, 1)
            dve.wait_ge(s_setB, SETB)
            dve.sem_inc(y_copied, 1)

            def relu_block(j):
                nc.vector.tensor_scalar(relu[:, j, :], bankU[:, P * j:P * j + P],
                                        b1[:, j:j + 1], 0.0, ALU.add, ALU.max).then_inc(relu_done, 1)

            with dve.Fori(0, ITER) as i:
                for s in range(STEPS):
                    p, t = s // CH, s % CH
                    step(1, s, i * STEPS + s)
                    c = i * 2 + p
                    if t == 2:
                        dve.wait_ge(u_ready, c + 1)
                        relu_block(0)
                        relu_block(1)
                    if t == 3:
                        relu_block(2)
                        relu_block(3)
                    if t == 6:
                        dve.wait_ge(y_stored[1 - p], i * 16 + 16)
                        dve.wait_ge(y_ready, c + 1)
                        nc.vector.tensor_tensor(out=y_sb[:, 1 - p, :], in0=bankY[:, 0:D], in1=b2[:],
                                                op=ALU.add).then_inc(y_copied, 1)
            for j in range(4):
                if j == 0:
                    dve.wait_ge(u_ready, NCH + 1)
                relu_block(j)
            dve.wait_ge(y_stored[1], 16 * ITER + 16)
            dve.wait_ge(y_ready, NCH + 1)
            nc.vector.tensor_tensor(out=y_sb[:, 1, :], in0=bankY[:, 0:D], in1=b2[:], op=ALU.add).then_inc(y_copied, 1)


_INS = ['x', 'cond_1024', 'L0_cond_Wx', 'L0_cond_Wh', 'L0_cond_b', 'L0_attn_W_theta', 'L0_attn_W_phi', 'L0_attn_W_g',
        'L0_cond2_Wx', 'L0_cond2_Wh', 'L0_cond2_b', 'L0_ffn_W1', 'L0_ffn_b1', 'L0_ffn_W2', 'L0_ffn_b2']


def kernel(**inputs):
    import numpy as _np
    import concourse.bacc as _bacc
    from concourse import mybir as _mybir
    from concourse.bass_utils import run_bass_kernel_spmd as _run

    nc = _bacc.Bacc("TRN2", target_bir_lowering=False, num_devices=1)
    arrays, args = {}, []
    for name in _INS:
        a = _np.ascontiguousarray(inputs[name])
        arrays[f"in_{name}_dram"] = a
        args.append(nc.dram_tensor(f"in_{name}_dram", a.shape, _mybir.dt.from_np(a.dtype), kind="ExternalInput").ap())
    x = inputs['x']
    out = nc.dram_tensor("out_0_dram", tuple(x.shape), _mybir.dt.float32, kind="ExternalOutput").ap()
    build(nc, *args, out)
    r = _run(nc, [arrays], core_ids=[0])
    return r.results[0]["out_0_dram"]
```

```python
import math
from contextlib import ExitStack

import concourse.bass as bass
from concourse import mybir


def build(nc, x, cond, l1_wx, l1_wh, l1_b, w_theta, w_phi, w_g,
          l2_wx, l2_wh, l2_b, f_w1, f_b1, f_w2, f_b2, out):
    f32 = mybir.dt.float32
    bf16 = mybir.dt.bfloat16
    f16 = mybir.dt.float16
    ALU = mybir.AluOpType
    ACT = mybir.ActivationFunctionType

    NB, T, D = x.shape
    H = D
    LAT = w_theta.shape[0]
    P = 128
    CH = P // NB
    NCH = T // CH
    ITER = NCH // 2
    STEPS = 2 * CH
    NJ = f_w1.shape[1] // P
    WARM1 = [2, 1, 1, 2, 2, 2, 2, 3]
    WARM2 = [1, 1, 0, 1, 1, 1, 1, 1]
    GI, GF, GO, GG = range(4)
    FIG = [GG, GF, GI]
    HS = 2.0 ** 14
    H_UNIT = 2.0 * HS
    SC_OUT = 1.0 / math.sqrt(D)

    ctx = ExitStack()
    with ctx:
        def sb(name, shape, dt=f32):
            return ctx.enter_context(nc.sbuf_tensor(name, shape, dt))

        def ps(name):
            return ctx.enter_context(nc.psum_tensor(name, [P, 512], f32))

        def sem(name):
            return ctx.enter_context(nc.semaphore(name))

        x_rows = sb("x_rows", [P, 2, D])
        xT = sb("xT", [P, NCH + 1, P])
        x2T = sb("x2T", [P, NCH + 1, P])
        xin = sb("xin", [P, 2, P])
        xres = sb("xres", [P, 2, P])
        ident = sb("ident", [P, P])
        ones = sb("ones", [P, P])
        wx = [sb(f"wx{n}", [P, 4 * H]) for n in (1, 2)]
        wh = [sb(f"wh{n}", [P, 4 * H]) for n in (1, 2)]
        bias = [sb(f"bias{n}", [P, 4 * H]) for n in (1, 2)]
        cond_rows = sb("cond_rows", [NB, H])
        h0 = sb("h0", [P, NB])
        wh_parts = [sb(f"wh_parts{n}", [P, 3, 4 * H], bf16) for n in (1, 2)]
        wh_rest = [sb(f"wh_rest{n}", [P, 4 * H]) for n in (1, 2)]
        wtp = sb("wtp", [P, 2, D])
        wg_rows = sb("wg_rows", [P, D])
        proj = sb("proj", [P, 2, D])
        w1 = sb("w1", [P, NJ * P])
        w2 = sb("w2", [P, NJ, D])
        b1 = sb("b1", [P, NJ])
        b2 = sb("b2", [P, D])
        gates = sb("gates", [P, 2, 4 * NB])
        ogate = sb("ogate", [P, NB])
        ogate1 = sb("ogate1", [P, NB])
        h_hi = sb("h_hi", [P, STEPS, NB], f16)
        h_lo = sb("h_lo", [P, STEPS, NB], f16)
        prods = sb("prods", [P, 2 * NB])
        warm = sb("warm", [P, 1])
        warm_w = sb("warm_w", [P, P], bf16)
        warm_x = sb("warm_x", [P, 512], bf16)
        ring = sb("ring", [P, STEPS, NB])
        hist = sb("hist", [P, NCH, P])
        rows = sb("rows", [P, 2, 2 * D])
        rows_t = sb("rows_t", [P, NB, 2 * D])
        pb = sb("pb", [P, NB, D])
        relu = sb("relu", [P, NJ, P])
        y_sb = sb("y_sb", [P, 2, D])

        fig = [ps("fig0"), ps("fig1")]
        ob = [ps("ob0"), ps("ob1")]
        cell = ps("cell")
        bankU, bankV, bankY = ps("bankU"), ps("bankV"), ps("bankY")
        c_psum, tanhc = cell[:, 0:NB], cell[:, NB:2 * NB]

        s_id = sem("s_id")
        s_w2l = sem("s_w2l")
        s_x0 = sem("s_x0")
        rows_loaded = [sem("rows_loaded0"), sem("rows_loaded1")]
        x_tr = sem("x_tr")
        x_cp = sem("x_cp")
        cond_tr = sem("cond_tr")
        wtp_cleared = sem("wtp_cleared")
        bias1_cleared = sem("bias1_cleared")
        s_attn_w = sem("s_attn_w")
        proj_mm = sem("proj_mm")
        s_const = sem("s_const")
        wx_ready = sem("wx_ready")
        wh_ready = sem("wh_ready")
        bias_ready = sem("bias_ready")
        s_wx1 = sem("s_wx1")
        s_wh1 = sem("s_wh1")
        s_b1 = sem("s_b1")
        s_setA = sem("s_setA")
        s_setB = sem("s_setB")
        h0_done = sem("h0_done")
        bankY_read = sem("bankY_read")
        fig_ready = [sem("fig_ready1"), sem("fig_ready2")]
        o_ready = [sem("o_ready1"), sem("o_ready2")]
        gates_done = [sem("gates_done1"), sem("gates_done2")]
        tanh_done = [sem("tanh_done1"), sem("tanh_done2")]
        prod_done = [sem("prod_done1"), sem("prod_done2")]
        c_ready = [sem("c_ready1"), sem("c_ready2")]
        h_ready = [sem("h_ready1"), sem("h_ready2")]
        hi_ready = [sem("hi_ready1"), sem("hi_ready2")]
        lo_ready = [sem("lo_ready1"), sem("lo_ready2")]
        s_part = [sem("s_part1"), sem("s_part2")]
        hist_done = sem("hist_done")
        rows_ready = sem("rows_ready")
        rows_moved = [sem("rows_moved0"), sem("rows_moved1")]
        outer_ready = sem("outer_ready")
        pb_kept = sem("pb_kept")
        attn_ready = sem("attn_ready")
        x2_first = sem("x2_first")
        x2_done = sem("x2_done")
        xin_loaded = [sem("xin_loaded0"), sem("xin_loaded1")]
        xres_loaded = [sem("xres_loaded0"), sem("xres_loaded1")]
        xp_done = sem("xp_done")
        u_ready = sem("u_ready")
        relu_done = sem("relu_done")
        relu_act = sem("relu_act")
        y_ready = sem("y_ready")
        y_copied = sem("y_copied")
        y_stored = [sem("y_stored0"), sem("y_stored1")]

        block = ctx.enter_context(nc.Block())

        def gate_cols(g):
            return slice(g * H, (g + 1) * H)

        x_ctb = x.rearrange("b (c t) d -> c t b d", t=CH)
        out_tb = out.rearrange("b (c t) d -> c t b d", t=CH)

        def split_wh(eng, e, layer):
            done, w, parts, rest = s_part[layer], wh[layer], wh_parts[layer], wh_rest[layer]
            e.tensor_scalar(parts[:, 0, :], w[:], 1.0 / H_UNIT, None, ALU.mult).then_inc(done, 1)
            eng.wait_ge(done, 1)
            if layer == 0:
                e.scalar_tensor_tensor(out=rest[:], in0=w[:], scalar=1.0 / H_UNIT, in1=parts[:, 0, :],
                                       op0=ALU.mult, op1=ALU.subtract).then_inc(done, 1)
            else:
                e.tensor_scalar(rest[:], w[:], 1.0 / H_UNIT, None, ALU.mult).then_inc(done, 1)
                eng.wait_ge(done, 2)
                e.tensor_tensor(out=rest[:], in0=rest[:], in1=parts[:, 0, :], op=ALU.subtract).then_inc(done, 1)
            eng.wait_ge(done, 2 + layer)
            e.tensor_copy(parts[:, 1, :], rest[:]).then_inc(done, 1)
            eng.wait_ge(done, 3 + layer)
            e.tensor_tensor(out=parts[:, 2, :], in0=rest[:], in1=parts[:, 1, :], op=ALU.subtract).then_inc(done, 1)

        def start_h(layer):
            nc.vector.memset(h_hi[:, STEPS - 1, :], 0.0).then_inc(hi_ready[layer], 1)
            nc.vector.memset(h_lo[:, STEPS - 1, :], 0.0).then_inc(lo_ready[layer], 1)
            nc.vector.memset(gates[:, 0, 0:NB], 0.0)

        @block.sync
        def _(sp):
            sp.dma_start(x_rows[:, 0, :], x_ctb[0]).then_inc(rows_loaded[0], 16)
            sp.dma_start(cond_rows[:], cond).then_inc(s_x0, 16)
            sp.dma_start(x_rows[:, 1, :], x_ctb[1]).then_inc(rows_loaded[1], 16)
            sp.sem_inc(rows_moved[0], 32)
            sp.sem_inc(rows_moved[1], 16)

            def move_rows(c, slot):
                sp.wait_ge(bankY_read, c + 3)
                sp.dma_start(rows_t[c * CH:(c + 1) * CH, :, :], rows[:, slot, :]).then_inc(rows_moved[slot], 16)

            for c in range(NCH):
                if c < NCH - 1:
                    sp.wait_ge(x_tr, c + 1)
                    sp.dma_start(x_rows[:, c % 2, :], x_ctb[min(c + 2, NCH - 1)]).then_inc(rows_loaded[c % 2], 16)
                if c >= 1:
                    move_rows(c - 1, c % 2)
            move_rows(NCH - 1, 0)
            sp.wait_ge(x2_done, NB // 4)
            sp.wait_ge(s_setB, 1)
            sp.dma_start(xres[:, 1, :], x2T[:, NCH, :]).then_inc(xres_loaded[1], 16)
            sp.sem_inc(y_stored[0], 16)
            sp.sem_inc(y_stored[1], 32)

            def bring(i, half):
                c = i * 2 + half
                if not (isinstance(c, int) and c == 0):
                    sp.wait_ge(y_ready, c)
                sp.dma_start(xres[:, half:half + 1, :], x2T[:, bass.ds(c, 1), :]).then_inc(xres_loaded[half], 16)
                if not (isinstance(c, int) and c == 0):
                    sp.wait_ge(xp_done, c)
                sp.dma_start(xin[:, 1 - half:2 - half, :], x2T[:, bass.ds(c + 1, 1), :]).then_inc(xin_loaded[1 - half], 16)

            def store(c, slot, count):
                sp.wait_ge(y_copied, count + 1)
                sp.dma_start(out_tb[c], y_sb[:, slot, :]).then_inc(y_stored[slot], 16)

            bring(0, 0)
            bring(0, 1)
            store(0, 0, 2)
            with sp.Fori(1, ITER) as i:
                bring(i, 0)
                c1 = sp.snap(i * 2 - 1)
                sp.wait_ge(y_copied, c1 + 3)
                sp.dma_start(out_tb[bass.ds(c1, 1)].rearrange("o t b d -> (o t) b d"), y_sb[:, 1, :]).then_inc(y_stored[1], 16)
                bring(i, 1)
                c2 = sp.snap(i * 2)
                sp.wait_ge(y_copied, c2 + 3)
                sp.dma_start(out_tb[bass.ds(c2, 1)].rearrange("o t b d -> (o t) b d"), y_sb[:, 0, :]).then_inc(y_stored[0], 16)
            store(NCH - 1, 1, NCH + 1)
            for slot in range(2):
                sp.wait_ge(y_stored[slot], 16 * (NCH // 2 + 1 + slot))

        SETB = 1 + 3 + 1

        @block.gpsimd
        def _(pool):
            nc.gpsimd.memset(ident[:], 0.0).then_inc(s_id, 1)
            pool.wait_ge(s_id, 1)
            nc.gpsimd.affine_select(out=ident[:], in_=ident[:], compare_op=ALU.not_equal, fill=1.0, base=0,
                                    pattern=[[-1, P]], channel_multiplier=1).then_inc(s_id, 1)
            nc.gpsimd.memset(wtp[:], 0.0).then_inc(wtp_cleared, 1)
            pool.wait_ge(wtp_cleared, 1)
            pool.dma_start(wtp[0:LAT, 0, :], w_theta).then_inc(s_attn_w, 16)
            pool.dma_start(wtp[0:LAT, 1, :], w_phi).then_inc(s_attn_w, 16)
            pool.dma_start(wg_rows[:], w_g).then_inc(s_attn_w, 16)
            nc.gpsimd.memset(bias[1][:], 0.0).then_inc(s_setA, 1)
            pool.wait_ge(s_setA, 1)
            pool.dma_start(bias[1][0:1, :], l2_b.unsqueeze(0)).then_inc(s_w2l, 16)
            pool.dma_start(wx[1][:], l2_wx).then_inc(s_w2l, 16)
            pool.dma_start(wh[1][:], l2_wh).then_inc(s_w2l, 16)
            pool.dma_start(w1[:], f_w1).then_inc(s_w2l, 16)
            pool.dma_start(w2[:], f_w2.rearrange("(j p) d -> p j d", p=P)).then_inc(s_w2l, 16)
            pool.dma_start(b1[:], f_b1.rearrange("(j p) -> p j", p=P), allow_slow_non_contiguous=True).then_inc(s_w2l, 16)
            pool.dma_start(b2[:], f_b2.unsqueeze(0).broadcast_to([P, D])).then_inc(s_w2l, 16)
            nc.gpsimd.memset(x2T[:, NCH, :], 0.0).then_inc(s_setB, 1)
            pool.wait_ge(s_w2l, 112)
            for w in (wx[1], wh[1], bias[1]):
                nc.gpsimd.tensor_scalar(w[:, gate_cols(GG)], w[:, gate_cols(GG)], 2.0, None, ALU.mult).then_inc(s_setB, 1)
            nc.gpsimd.tensor_scalar(w1[:], w1[:], 1.0 / H_UNIT, None, ALU.mult).then_inc(s_setB, 1)
            pool.wait_ge(s_setB, SETB)
            split_wh(pool, nc.gpsimd, 1)

        OUTER_BANKS = [bankU, cell, bankV, bankY]
        UP_BANKS = [bankU, cell, fig[0], ob[0]]

        @block.tensor
        def _(pe):
            def gate_out(p, g):
                if g == GO:
                    return ob[p][:, 0:P]
                return fig[p][:, 0:3 * P].rearrange("p (t g b) -> p t g b", g=3, b=NB)[:, :, FIG.index(g), :]

            def moving(tile, g):
                return tile if g == GO else tile.rearrange("p (t b) -> p t b", b=NB)

            def bias_gate(layer, p, g):
                return nc.tensor.matmul(gate_out(p, g), bias[layer][:, gate_cols(g)], moving(ones[:, :], g),
                                        start=g in (FIG[0], GO), stop=False, skip_group_check=True)

            def project_gate(layer, p, g, tile):
                return nc.tensor.matmul(gate_out(p, g), wx[layer][:, gate_cols(g)], moving(tile, g),
                                        start=False, stop=False, skip_group_check=True)

            def keep_warm(bank, n):
                for _ in range(n):
                    nc.tensor.matmul(bank[:, :], warm_w[:], warm_x[:], start=True, stop=True)

            def initial(layer):
                for g in FIG + [GO]:
                    dst = ob[0][:, 0:NB] if g == GO else fig[0][:, FIG.index(g) * NB:FIG.index(g) * NB + NB]
                    nc.tensor.matmul(dst, wh[layer][:, gate_cols(g)], h0[:], start=False, stop=True,
                                     skip_group_check=True)

            def step(layer, s, count):
                p, t = s // CH, s % CH
                def passes(h, gs):
                    for g in gs:
                        if g == GO:
                            dst = ob[p][:, NB * t:NB * t + NB]
                        else:
                            c0 = (3 * t + FIG.index(g)) * NB
                            dst = fig[p][:, c0:c0 + NB]
                        for part in range(3):
                            last = nc.tensor.matmul(dst, wh_parts[layer][:, part, gate_cols(g)],
                                                    h[:, (s - 1) % STEPS, :],
                                                    start=False, stop=True, skip_group_check=True)
                    return last

                pe.wait_ge(hi_ready[layer], count)
                passes(h_hi, FIG)
                pe.wait_ge(lo_ready[layer], count)
                passes(h_lo, FIG).then_inc(fig_ready[layer], 1)
                passes(h_hi, [GO])
                passes(h_lo, [GO]).then_inc(o_ready[layer], 1)

            pe.wait_ge(s_const, 1)
            keep_warm(bankV, 5)
            pe.wait_ge(s_const, 2)
            pe.wait_ge(s_id, 2)
            pe.wait_ge(rows_loaded[0], 16)
            nc.tensor.transpose(bankU[:, 0:P], x_rows[:, 0, :], ident[:]).then_inc(x_tr, 1)
            pe.wait_ge(s_x0, 16)
            nc.tensor.transpose(bankY[:, 0:NB], cond_rows[:], ident[0:NB, 0:NB]).then_inc(cond_tr, 1)
            keep_warm(bankV, 3)
            pe.wait_ge(bias_ready, 1)
            for g in FIG + [GO]:
                bias_gate(0, 0, g)
            pe.wait_ge(h0_done, 1)
            pe.wait_ge(wh_ready, 1)
            initial(0)
            pe.wait_ge(x_cp, 1)
            pe.wait_ge(wx_ready, 1)
            for g in FIG + [GO]:
                project_gate(0, 0, g, xT[:, 0, :])
            pe.wait_ge(s_attn_w, 48)
            nc.tensor.matmul(bankY[:, 0:P], wtp[:, 1, :], wtp[:, 0, :], start=True, stop=True)
            nc.tensor.transpose(bankY[:, P:2 * P], wg_rows[:], ident[:]).then_inc(proj_mm, 1)
            pe.wait_ge(s_part[0], 4)

            def row_products(half):
                nc.tensor.matmul(bankY[:, 0:2 * D], ring[:, CH * half:CH * half + CH, :].rearrange("p t b -> p (t b)"),
                                 proj[:].rearrange("p a n -> p (a n)"), start=True, stop=True).then_inc(rows_ready, 1)

            with pe.Fori(0, ITER) as i:
                for s in range(STEPS):
                    p, t = s // CH, s % CH
                    step(0, s, i * STEPS + (s + 1))
                    if t == 0:
                        pe.wait_ge(rows_loaded[1 - p], i * 16 + 16 * (p + 1))
                        nc.tensor.transpose(bankU[:, 0:P], x_rows[:, 1 - p, :], ident[:]).then_inc(x_tr, 1)
                        pe.wait_ge(bankY_read, i * 2 + (p + 1))
                        row_products(1 - p)
                    if t in (1, 2):
                        for g in ((FIG[0], FIG[1]), (FIG[2], GO))[t - 1]:
                            bias_gate(0, 1 - p, g)
                    if t == 3:
                        pe.wait_ge(x_cp, i * 2 + (p + 2))
                    if t in (3, 4, 5, 6):
                        rhs = xT[:, bass.ds(i * 2 + (p + 1), 1), :].rearrange("p c n -> p (c n)")
                        project_gate(0, 1 - p, (FIG + [GO])[t - 3], rhs)
                    keep_warm(bankV, WARM1[t])

            pe.wait_ge(h_ready[0], T)
            pe.wait_ge(bankY_read, NCH + 1)
            row_products(1)
            pe.wait_ge(s_setB, SETB)
            for g in FIG + [GO]:
                bias_gate(1, 0, g)
            initial(1)
            keep_warm(bankV, 4)
            pe.wait_ge(bankY_read, NCH + 2)
            pe.wait_ge(hist_done, NCH)
            pe.wait_ge(rows_moved[1], 16 * (ITER + 1))
            pe.wait_ge(rows_moved[0], 16 * (ITER + 2))

            def outer_pair(q):
                if q >= len(OUTER_BANKS):
                    pe.wait_ge(pb_kept, q - len(OUTER_BANKS) + 1)
                for k in range(2):
                    last = nc.tensor.matmul(OUTER_BANKS[q % len(OUTER_BANKS)][:, P * k:P * k + P],
                                            rows_t[:, 2 * q + k, 0:D], rows_t[:, 2 * q + k, D:2 * D],
                                            start=True, stop=True)
                last.then_inc(outer_ready, 1)

            hist_b = hist[:].rearrange("p c (t b) -> p b (c t)", b=NB)

            def attend_pair(q):
                pe.wait_ge(pb_kept, q + 1)
                if q >= 4 and q % 2 == 0:
                    pe.wait_ge(x2_done, q // 2 - 1)
                for k in range(2):
                    c0 = P * (2 * (q % 2) + k)
                    last = nc.tensor.matmul((fig[1], ob[1])[q // 2 % 2][:, c0:c0 + P], pb[:, 2 * q + k, :],
                                            hist_b[:, 2 * q + k, :], start=True, stop=True)
                last.then_inc(attn_ready, 1)

            PAIRS = NB // 2
            for q in range(PAIRS + 2):
                if q < PAIRS:
                    outer_pair(q)
                if q >= 2:
                    attend_pair(q - 2)

            pe.wait_ge(x2_first, NB // 4)
            for g in FIG + [GO]:
                last = project_gate(1, 0, g, x2T[:, 0, :])
            last.then_inc(xp_done, 1)
            pe.wait_ge(s_part[1], 5)

            def ffn_up(half, j, bank=bankU):
                return nc.tensor.matmul(bank[:, P * j:P * j + P],
                                        w1[:, j * P:j * P + P],
                                        ring[:, CH * half:CH * half + CH, :].rearrange("p t b -> p (t b)"),
                                        start=True, stop=True)

            def ffn_down(j):
                return nc.tensor.matmul(bankY[:, 0:D], relu[:, j, :], w2[:, j, :], start=False, stop=(j == NJ - 1))

            def residual(half):
                return nc.tensor.matmul(bankY[:, 0:D], xres[:, half, :], ident[:], start=True, stop=False)

            with pe.Fori(0, ITER) as i:
                for s in range(STEPS):
                    p, t = s // CH, s % CH
                    step(1, s, i * STEPS + (s + 1))
                    c = i * 2 + p
                    if t == 0:
                        for j in range(2):
                            ffn_up(1 - p, j)
                    if t == 1:
                        for j in range(2, 4):
                            last = ffn_up(1 - p, j)
                        last.then_inc(u_ready, 1)
                    if t == 2:
                        pe.wait_ge(xres_loaded[1 - p], i * 16 + 16)
                        pe.wait_ge(y_copied, c + 1)
                        residual(1 - p)
                    if t == 4:
                        pe.wait_ge(relu_done, c * 4 + 2)
                        ffn_down(0)
                        ffn_down(1)
                    if t == 5:
                        pe.wait_ge(relu_done, c * 4 + 4)
                        ffn_down(2)
                        ffn_down(3).then_inc(y_ready, 1)
                    if t == 2:
                        pe.wait_ge(xin_loaded[1 - p], i * 16 + 16)
                    if t in (2, 3, 6, 7):
                        g = {2: FIG[0], 3: FIG[1], 6: FIG[2], 7: GO}[t]
                        bias_gate(1, 1 - p, g)
                        last = project_gate(1, 1 - p, g, xin[:, 1 - p, :])
                    if t == 7:
                        last.then_inc(xp_done, 1)
                    keep_warm(bankV, WARM2[t])
            pe.wait_ge(xres_loaded[1], 16 * (ITER + 1))
            pe.wait_ge(y_copied, NCH + 1)
            residual(1)
            pe.wait_ge(h_ready[1], T)
            for j in range(NJ):
                ffn_up(1, j, UP_BANKS[j]).then_inc(u_ready, 1)
            for j in range(NJ):
                pe.wait_ge(*((relu_done, 4 * NCH + 1 + j // 2), (relu_act, 1 + j // 2))[j % 2])
                last = ffn_down(j)
            last.then_inc(y_ready, 1)

        @block.scalar
        def _(act):
            act.dma_start(wh[0][:], l1_wh).then_inc(s_wh1, 16)
            act.dma_start(wx[0][:], l1_wx).then_inc(s_wx1, 16)
            act.wait_ge(bias1_cleared, 1)
            act.dma_start(bias[0][0:1, :], l1_b.unsqueeze(0)).then_inc(s_b1, 16)
            act.wait_ge(s_id, 2)
            nc.scalar.activation(warm[:], ident[:, 0:1], ACT.Tanh)
            act.wait_ge(x_tr, 1)
            nc.scalar.copy(xT[:, 0, :], bankU[:, 0:P]).then_inc(x_cp, 1)
            act.wait_ge(cond_tr, 1)
            nc.scalar.copy(h0[:], bankY[:, 0:NB]).then_inc(h0_done, 1)
            act.wait_ge(proj_mm, 1)
            nc.scalar.mul(proj[:, 0, :], bankY[:, 0:P], SC_OUT / H_UNIT ** 2)
            nc.scalar.mul(proj[:, 1, :], bankY[:, P:2 * P], 1.0 / H_UNIT).then_inc(bankY_read, 1)

            def step(layer, s, n):
                p, t = s // CH, s % CH
                n1 = n + 1
                act.wait_ge(fig_ready[layer], n1)
                nc.scalar.activation(gates[:, s % 2, NB:4 * NB], fig[p][:, 3 * NB * t:3 * NB * (t + 1)],
                                     ACT.Tanh, scale=0.5).then_inc(gates_done[layer], 1)
                act.wait_ge(o_ready[layer], n1)
                nc.scalar.activation(ogate[:], ob[p][:, NB * t:NB * t + NB], ACT.Tanh,
                                     scale=0.5).then_inc(tanh_done[layer], 1)
                act.wait_ge(tanh_done[layer], n * 3 + 1)
                nc.scalar.activation(ogate1[:], ogate[:], ACT.Identity, bias=HS, scale=HS).then_inc(tanh_done[layer], 1)
                act.wait_ge(c_ready[layer], n1)
                nc.scalar.activation(tanhc, c_psum, ACT.Tanh,
                                     scale=0.5).then_inc(tanh_done[layer], 1)

            def keep_rows(slot, i, c):
                act.wait_ge(rows_moved[slot], i * 16 + 16)
                act.wait_ge(rows_ready, c + 1)
                nc.scalar.copy(rows[:, slot, :], bankY[:, 0:2 * D]).then_inc(bankY_read, 1)

            with act.Fori(0, ITER) as i:
                for s in range(STEPS):
                    step(0, s, i * STEPS + s)
                    p, t = s // CH, s % CH
                    if t == 1:
                        c = act.snap(i * 2 + (p + 1))
                        act.wait_ge(x_tr, i * 2 + (p + 2))
                        nc.scalar.copy(xT[:, bass.ds(c, 1), :].rearrange("p c n -> p (c n)"),
                                       bankU[:, 0:P]).then_inc(x_cp, 1)
                    if t == 2:
                        keep_rows(p, i, i * 2 + p)
            keep_rows(0, ITER, NCH)
            for q in range(NB // 2):
                act.wait_ge(outer_ready, q + 1)
                nc.scalar.copy(pb[:, 2 * q:2 * q + 2, :].rearrange("p a n -> p (a n)"),
                               OUTER_BANKS[q % len(OUTER_BANKS)][:, 0:2 * D]).then_inc(pb_kept, 1)
            with act.Fori(0, ITER) as i:
                for s in range(STEPS):
                    step(1, s, i * STEPS + s)
            for j in (1, 3):
                act.wait_ge(u_ready, NCH + 1 + j)
                nc.scalar.activation(relu[:, j, :], UP_BANKS[j][:, P * j:P * j + P], ACT.Relu,
                                     bias=b1[:, j:j + 1]).then_inc(relu_act, 1)

        @block.vector
        def _(dve):
            nc.vector.memset(bias[0][:], 0.0).then_inc(bias1_cleared, 1)
            nc.vector.memset(warm_w[:], 1.0)
            nc.vector.memset(warm_x[:], 1.0).then_inc(s_const, 1)
            nc.vector.memset(ones[:], 1.0).then_inc(s_const, 1)
            nc.vector.memset(ring[:, CH:STEPS, :], 0.0)
            start_h(0)
            dve.wait_ge(s_wh1, 16)
            nc.vector.tensor_scalar(wh[0][:, gate_cols(GG)], wh[0][:, gate_cols(GG)], 2.0, None,
                                    ALU.mult).then_inc(wh_ready, 1)
            dve.wait_ge(s_b1, 16)
            nc.vector.tensor_scalar(bias[0][:, gate_cols(GG)], bias[0][:, gate_cols(GG)], 2.0, None,
                                    ALU.mult).then_inc(bias_ready, 1)
            dve.wait_ge(s_wx1, 16)
            nc.vector.tensor_scalar(wx[0][:, gate_cols(GG)], wx[0][:, gate_cols(GG)], 2.0, None,
                                    ALU.mult).then_inc(wx_ready, 1)
            dve.wait_ge(wh_ready, 1)
            split_wh(dve, nc.vector, 0)

            def step(layer, s, n):
                p = s % 2
                n1 = n + 1
                dve.wait_ge(gates_done[layer], n1)
                nc.vector.scalar_tensor_tensor(out=prods[:], in0=gates[:, p, 2 * NB:4 * NB], scalar=1.0,
                                               in1=gates[:, p, 0:2 * NB], op0=ALU.add,
                                               op1=ALU.mult).then_inc(prod_done[layer], 1)
                dve.wait_ge(prod_done[layer], n1)
                nc.vector.scalar_tensor_tensor(out=c_psum, in0=prods[:, 0:NB], scalar=0.5,
                                               in1=prods[:, NB:2 * NB], op0=ALU.mult,
                                               op1=ALU.add).then_inc(c_ready[layer], 1)
                nc.vector.scalar_tensor_tensor(out=gates[:, 1 - p, 0:NB], in0=prods[:, 0:NB], scalar=0.5,
                                               in1=prods[:, NB:2 * NB], op0=ALU.mult,
                                               op1=ALU.add)
                dve.wait_ge(tanh_done[layer], n * 3 + 3)
                nc.vector.tensor_tensor(out=h_hi[:, s, :], in0=ogate1[:], in1=tanhc,
                                        op=ALU.mult).then_inc(hi_ready[layer], 1)
                nc.vector.tensor_tensor(out=ring[:, s, :], in0=ogate1[:], in1=tanhc,
                                        op=ALU.mult).then_inc(h_ready[layer], 1)
                dve.wait_ge(h_ready[layer], n1)
                nc.vector.tensor_tensor(out=h_lo[:, s, :], in0=ring[:, s, :], in1=h_hi[:, s, :],
                                        op=ALU.subtract).then_inc(lo_ready[layer], 1)

            with dve.Fori(0, ITER) as i:
                for s in range(STEPS):
                    step(0, s, i * STEPS + s)
                    p, t = s // CH, s % CH
                    if t == CH - 1:
                        c = dve.snap(i * 2 + p)
                        nc.vector.tensor_copy(hist[:, bass.ds(c, 1), :].rearrange("p c n -> p (c n)"),
                                              ring[:, CH * p:CH * p + CH, :].rearrange("p t b -> p (t b)")
                                              ).then_inc(hist_done, 1)
            dve.wait_ge(lo_ready[0], T + 1)
            start_h(1)
            xb = xT[:, 0:NCH, :].rearrange("p c (t b) -> p b c t", b=NB)
            x2b = x2T[:, 0:NCH, :].rearrange("p c (t b) -> p b c t", b=NB)
            for q in range(NB // 4):
                dve.wait_ge(attn_ready, 2 * q + 2)
                o = (fig[1], ob[1])[q % 2][:, :].rearrange("p (b n) -> p b n", b=4)
                b4 = slice(4 * q, 4 * q + 4)
                nc.vector.tensor_tensor(out=x2b[:, b4, 0, :], in0=o[:, :, 0:CH], in1=xb[:, b4, 0, :],
                                        op=ALU.add).then_inc(x2_first, 1)
                nc.vector.tensor_tensor(out=x2b[:, b4, 1:NCH, :],
                                        in0=o[:, :, CH:T].rearrange("p b (c t) -> p b c t", t=CH),
                                        in1=xb[:, b4, 1:NCH, :], op=ALU.add).then_inc(x2_done, 1)
            dve.wait_ge(s_setB, SETB)
            dve.sem_inc(y_copied, 1)

            def relu_block(j, bank=bankU):
                nc.vector.tensor_scalar(relu[:, j, :], bank[:, P * j:P * j + P],
                                        b1[:, j:j + 1], 0.0, ALU.add, ALU.max).then_inc(relu_done, 1)

            with dve.Fori(0, ITER) as i:
                for s in range(STEPS):
                    p, t = s // CH, s % CH
                    step(1, s, i * STEPS + s)
                    c = i * 2 + p
                    if t == 2:
                        dve.wait_ge(u_ready, c + 1)
                        relu_block(0)
                        relu_block(1)
                    if t == 3:
                        relu_block(2)
                        relu_block(3)
                    if t == 6:
                        dve.wait_ge(y_stored[1 - p], i * 16 + 16)
                        dve.wait_ge(y_ready, c + 1)
                        nc.vector.tensor_tensor(out=y_sb[:, 1 - p, :], in0=bankY[:, 0:D], in1=b2[:],
                                                op=ALU.add).then_inc(y_copied, 1)
            for j in (0, 2):
                dve.wait_ge(u_ready, NCH + 1 + j)
                relu_block(j, UP_BANKS[j])
            dve.wait_ge(y_stored[1], 16 * ITER + 16)
            dve.wait_ge(y_ready, NCH + 1)
            nc.vector.tensor_tensor(out=y_sb[:, 1, :], in0=bankY[:, 0:D], in1=b2[:], op=ALU.add).then_inc(y_copied, 1)


_INS = ['x', 'cond_1024', 'L0_cond_Wx', 'L0_cond_Wh', 'L0_cond_b', 'L0_attn_W_theta', 'L0_attn_W_phi', 'L0_attn_W_g',
        'L0_cond2_Wx', 'L0_cond2_Wh', 'L0_cond2_b', 'L0_ffn_W1', 'L0_ffn_b1', 'L0_ffn_W2', 'L0_ffn_b2']


def kernel(**inputs):
    import numpy as _np
    import concourse.bacc as _bacc
    from concourse import mybir as _mybir
    from concourse.bass_utils import run_bass_kernel_spmd as _run

    nc = _bacc.Bacc("TRN2", target_bir_lowering=False, num_devices=1)
    arrays, args = {}, []
    for name in _INS:
        a = _np.ascontiguousarray(inputs[name])
        arrays[f"in_{name}_dram"] = a
        args.append(nc.dram_tensor(f"in_{name}_dram", a.shape, _mybir.dt.from_np(a.dtype), kind="ExternalInput").ap())
    x = inputs['x']
    out = nc.dram_tensor("out_0_dram", tuple(x.shape), _mybir.dt.float32, kind="ExternalOutput").ap()
    build(nc, *args, out)
    r = _run(nc, [arrays], core_ids=[0])
    return r.results[0]["out_0_dram"]
```

```python
import math
from contextlib import ExitStack

import concourse.bass as bass
from concourse import mybir


def build(nc, x, cond, l1_wx, l1_wh, l1_b, w_theta, w_phi, w_g,
          l2_wx, l2_wh, l2_b, f_w1, f_b1, f_w2, f_b2, out):
    f32 = mybir.dt.float32
    bf16 = mybir.dt.bfloat16
    f16 = mybir.dt.float16
    ALU = mybir.AluOpType
    ACT = mybir.ActivationFunctionType

    NB, T, D = x.shape
    H = D
    LAT = w_theta.shape[0]
    P = 128
    CH = P // NB
    NCH = T // CH
    ITER = NCH // 2
    STEPS = 2 * CH
    NJ = f_w1.shape[1] // P
    WARM1 = [0, 0, 0, 0, 1, 3, 1, 3]
    WARM2 = [1, 1, 0, 1, 1, 1, 1, 1]
    GI, GF, GO, GG = range(4)
    FIG = [GG, GF, GI]
    HS = 2.0 ** 14
    H_UNIT = 2.0 * HS
    SC_OUT = 1.0 / math.sqrt(D)

    ctx = ExitStack()
    with ctx:
        def sb(name, shape, dt=f32):
            return ctx.enter_context(nc.sbuf_tensor(name, shape, dt))

        def ps(name):
            return ctx.enter_context(nc.psum_tensor(name, [P, 512], f32))

        def sem(name):
            return ctx.enter_context(nc.semaphore(name))

        x_rows = sb("x_rows", [P, 2, D])
        xT = sb("xT", [P, NCH + 1, P])
        x2T = sb("x2T", [P, NCH + 1, P])
        xin = sb("xin", [P, 2, P])
        xres = sb("xres", [P, 2, P])
        ident = sb("ident", [P, P])
        ones = sb("ones", [P, P])
        wx = [sb(f"wx{n}", [P, 4 * H]) for n in (1, 2)]
        wh = [sb(f"wh{n}", [P, 4 * H]) for n in (1, 2)]
        bias = [sb(f"bias{n}", [P, 4 * H]) for n in (1, 2)]
        cond_rows = sb("cond_rows", [NB, H])
        h0 = sb("h0", [P, NB])
        wh_parts = [sb(f"wh_parts{n}", [P, 3, 4 * H], bf16) for n in (1, 2)]
        wh_rest = [sb(f"wh_rest{n}", [P, 4 * H]) for n in (1, 2)]
        wtp = sb("wtp", [P, 2, D])
        wg_rows = sb("wg_rows", [P, D])
        proj = sb("proj", [P, 2, D])
        w1 = sb("w1", [P, NJ * P])
        w2 = sb("w2", [P, NJ, D])
        b1 = sb("b1", [P, NJ])
        b2 = sb("b2", [P, D])
        gates = sb("gates", [P, 2, 4 * NB])
        ogate = sb("ogate", [P, NB])
        ogate1 = sb("ogate1", [P, NB])
        h_hi = sb("h_hi", [P, STEPS, NB], f16)
        h_lo = sb("h_lo", [P, STEPS, NB], f16)
        prods = sb("prods", [P, 2 * NB])
        warm = sb("warm", [P, 1])
        warm_w = sb("warm_w", [P, P], bf16)
        warm_x = sb("warm_x", [P, 512], bf16)
        zeros = sb("zeros", [P, 2 * P], bf16)
        ring = sb("ring", [P, STEPS, NB])
        hist = sb("hist", [P, NCH, P])
        rows = sb("rows", [P, 2, 2 * D])
        rows_t = sb("rows_t", [P, NB, 2 * D])
        rows0 = sb("rows0", [P, D])
        proj_at = sb("proj_at", [P, D])
        queries = sb("queries", [P, 2 * P])
        batch_of = sb("batch_of", [NB, P])
        same_batch = sb("same_batch", [P, 2 * P])
        scores = sb("scores", [P, 2 * P])
        p_batch = sb("p_batch", [P, NB, D])
        relu = sb("relu", [P, NJ, P])
        y_sb = sb("y_sb", [P, 2, D])

        figbank = [ps("figbank0"), ps("figbank1")]
        obank = [ps("obank0"), ps("obank1")]
        cell = ps("cell")
        bankU, bankV, bankY = ps("bankU"), ps("bankV"), ps("bankY")
        c_psum, tanhc = cell[:, 0:NB], cell[:, NB:2 * NB]

        ident_ready = sem("ident_ready")
        weights2_loaded = sem("weights2_loaded")
        cond_loaded = sem("cond_loaded")
        rows_loaded = [sem("rows_loaded0"), sem("rows_loaded1")]
        x_transposed = sem("x_transposed")
        xT_kept = sem("xT_kept")
        cond_transposed = sem("cond_transposed")
        wtp_cleared = sem("wtp_cleared")
        bias1_cleared = sem("bias1_cleared")
        attn_w_loaded = sem("attn_w_loaded")
        proj_ready = sem("proj_ready")
        consts_ready = sem("consts_ready")
        wx_ready = sem("wx_ready")
        wh_ready = sem("wh_ready")
        bias_ready = sem("bias_ready")
        wx1_loaded = sem("wx1_loaded")
        wh1_loaded = sem("wh1_loaded")
        bias1_loaded = sem("bias1_loaded")
        bias2_cleared = sem("bias2_cleared")
        set2_ready = sem("set2_ready")
        h0_kept = sem("h0_kept")
        rows_kept = sem("rows_kept")
        fig_ready = [sem("fig_ready1"), sem("fig_ready2")]
        o_ready = [sem("o_ready1"), sem("o_ready2")]
        gates_done = [sem("gates_done1"), sem("gates_done2")]
        tanh_done = [sem("tanh_done1"), sem("tanh_done2")]
        prod_done = [sem("prod_done1"), sem("prod_done2")]
        c_ready = [sem("c_ready1"), sem("c_ready2")]
        h_ready = [sem("h_ready1"), sem("h_ready2")]
        hi_ready = [sem("hi_ready1"), sem("hi_ready2")]
        lo_ready = [sem("lo_ready1"), sem("lo_ready2")]
        parts_ready = [sem("parts_ready1"), sem("parts_ready2")]
        hist_done = sem("hist_done")
        rows_ready = sem("rows_ready")
        rows_moved = [sem("rows_moved0"), sem("rows_moved1")]
        outer_ready = sem("outer_ready")
        p_kept = sem("p_kept")
        late_attn_ready = sem("late_attn_ready")
        batch_ready = sem("batch_ready")
        queries_ready = sem("queries_ready")
        queries_kept = sem("queries_kept")
        scores_ready = sem("scores_ready")
        scores_kept = sem("scores_kept")
        rows0_ready = sem("rows0_ready")
        rows0_kept = sem("rows0_kept")
        early_attn_ready = sem("early_attn_ready")
        x2_first = sem("x2_first")
        x2_done = sem("x2_done")
        xin_loaded = [sem("xin_loaded0"), sem("xin_loaded1")]
        xres_loaded = [sem("xres_loaded0"), sem("xres_loaded1")]
        x2_projected = sem("x2_projected")
        hidden_ready = sem("hidden_ready")
        relu_done = sem("relu_done")
        relu_act_done = sem("relu_act_done")
        y_ready = sem("y_ready")
        y_copied = sem("y_copied")
        y_stored = [sem("y_stored0"), sem("y_stored1")]

        block = ctx.enter_context(nc.Block())

        def gate_cols(g):
            return slice(g * H, (g + 1) * H)

        x_ctb = x.rearrange("b (c t) d -> c t b d", t=CH)
        out_tb = out.rearrange("b (c t) d -> c t b d", t=CH)

        def split_wh(eng, e, layer):
            done, w, parts, rest = parts_ready[layer], wh[layer], wh_parts[layer], wh_rest[layer]
            e.tensor_scalar(parts[:, 0, :], w[:], 1.0 / H_UNIT, None, ALU.mult).then_inc(done, 1)
            eng.wait_ge(done, 1)
            if layer == 0:
                e.scalar_tensor_tensor(out=rest[:], in0=w[:], scalar=1.0 / H_UNIT, in1=parts[:, 0, :],
                                       op0=ALU.mult, op1=ALU.subtract).then_inc(done, 1)
            else:
                e.tensor_scalar(rest[:], w[:], 1.0 / H_UNIT, None, ALU.mult).then_inc(done, 1)
                eng.wait_ge(done, 2)
                e.tensor_tensor(out=rest[:], in0=rest[:], in1=parts[:, 0, :], op=ALU.subtract).then_inc(done, 1)
            eng.wait_ge(done, 2 + layer)
            e.tensor_copy(parts[:, 1, :], rest[:]).then_inc(done, 1)
            eng.wait_ge(done, 3 + layer)
            e.tensor_tensor(out=parts[:, 2, :], in0=rest[:], in1=parts[:, 1, :], op=ALU.subtract).then_inc(done, 1)

        def start_h(layer):
            nc.vector.memset(h_hi[:, STEPS - 1, :], 0.0).then_inc(hi_ready[layer], 1)
            nc.vector.memset(h_lo[:, STEPS - 1, :], 0.0).then_inc(lo_ready[layer], 1)
            nc.vector.memset(gates[:, 0, 0:NB], 0.0)

        @block.sync
        def _(sp):
            sp.dma_start(x_rows[:, 0, :], x_ctb[0]).then_inc(rows_loaded[0], 16)
            sp.wait_ge(bias1_cleared, 1)
            sp.dma_start(bias[0][0:1, :], l1_b.unsqueeze(0)).then_inc(bias1_loaded, 16)
            sp.dma_start(cond_rows[:], cond).then_inc(cond_loaded, 16)
            sp.dma_start(x_rows[:, 1, :], x_ctb[1]).then_inc(rows_loaded[1], 16)
            sp.sem_inc(rows_moved[0], 32)
            sp.sem_inc(rows_moved[1], 16)

            def move_rows(c, slot):
                sp.wait_ge(rows_kept, c + 3)
                sp.dma_start(rows_t[c * CH:(c + 1) * CH, :, :], rows[:, slot, :]).then_inc(rows_moved[slot], 16)

            for c in range(NCH):
                if c < NCH - 1:
                    sp.wait_ge(x_transposed, c + 1)
                    sp.dma_start(x_rows[:, c % 2, :], x_ctb[min(c + 2, NCH - 1)]).then_inc(rows_loaded[c % 2], 16)
                if c >= 1:
                    move_rows(c - 1, c % 2)
            move_rows(NCH - 1, 0)
            sp.sem_inc(y_stored[0], 16)
            sp.sem_inc(y_stored[1], 32)
            for slot in range(2):
                sp.sem_inc(xres_loaded[slot], 16)
                sp.sem_inc(xin_loaded[slot], 16)
            sp.wait_ge(x2_done, NB // 4)

            def bring(i, half):
                c = i * 2 + half
                sp.wait_ge(y_ready, c)
                sp.dma_start(xres[:, half:half + 1, :], x2T[:, bass.ds(c, 1), :]).then_inc(xres_loaded[half], 16)
                sp.wait_ge(x2_projected, c)
                sp.dma_start(xin[:, 1 - half:2 - half, :], x2T[:, bass.ds(c + 1, 1), :]
                             ).then_inc(xin_loaded[1 - half], 16)

            def store(c, slot, count):
                sp.wait_ge(y_copied, count + 1)
                sp.dma_start(out_tb[c], y_sb[:, slot, :]).then_inc(y_stored[slot], 16)

            sp.dma_start(xres[:, 1, :], x2T[:, 1, :]).then_inc(xres_loaded[1], 16)
            store(0, 0, 2)
            with sp.Fori(1, ITER) as i:
                bring(i, 0)
                c1 = sp.snap(i * 2 - 1)
                sp.wait_ge(y_copied, c1 + 3)
                sp.dma_start(out_tb[bass.ds(c1, 1)].rearrange("o t b d -> (o t) b d"), y_sb[:, 1, :]
                             ).then_inc(y_stored[1], 16)
                bring(i, 1)
                c2 = sp.snap(i * 2)
                sp.wait_ge(y_copied, c2 + 3)
                sp.dma_start(out_tb[bass.ds(c2, 1)].rearrange("o t b d -> (o t) b d"), y_sb[:, 0, :]
                             ).then_inc(y_stored[0], 16)
            store(NCH - 1, 1, NCH + 1)
            for slot in range(2):
                sp.wait_ge(y_stored[slot], 16 * (NCH // 2 + 1 + slot))

        SET2 = 1 + 3 + 1

        @block.gpsimd
        def _(pool):
            nc.gpsimd.memset(ident[:], 0.0).then_inc(ident_ready, 1)
            pool.wait_ge(ident_ready, 1)
            nc.gpsimd.affine_select(out=ident[:], in_=ident[:], compare_op=ALU.not_equal, fill=1.0, base=0,
                                    pattern=[[-1, P]], channel_multiplier=1).then_inc(ident_ready, 1)
            nc.gpsimd.memset(wtp[:], 0.0).then_inc(wtp_cleared, 1)
            pool.wait_ge(wtp_cleared, 1)
            pool.dma_start(wtp[0:LAT, 0, :], w_theta).then_inc(attn_w_loaded, 16)
            pool.dma_start(wtp[0:LAT, 1, :], w_phi).then_inc(attn_w_loaded, 16)
            pool.dma_start(wg_rows[:], w_g).then_inc(attn_w_loaded, 16)
            nc.gpsimd.memset(bias[1][:], 0.0).then_inc(bias2_cleared, 1)
            pool.wait_ge(bias2_cleared, 1)
            pool.dma_start(bias[1][0:1, :], l2_b.unsqueeze(0)).then_inc(weights2_loaded, 16)
            pool.dma_start(wx[1][:], l2_wx).then_inc(weights2_loaded, 16)
            pool.dma_start(wh[1][:], l2_wh).then_inc(weights2_loaded, 16)
            pool.dma_start(w1[:], f_w1).then_inc(weights2_loaded, 16)
            pool.dma_start(w2[:], f_w2.rearrange("(j p) d -> p j d", p=P)).then_inc(weights2_loaded, 16)
            pool.dma_start(b1[:], f_b1.rearrange("(j p) -> p j", p=P),
                           allow_slow_non_contiguous=True).then_inc(weights2_loaded, 16)
            pool.dma_start(b2[:], f_b2.unsqueeze(0).broadcast_to([P, D])).then_inc(weights2_loaded, 16)
            nc.gpsimd.memset(x2T[:, NCH, :], 0.0).then_inc(set2_ready, 1)
            pool.wait_ge(weights2_loaded, 112)
            for w in (wx[1], wh[1], bias[1]):
                nc.gpsimd.tensor_scalar(w[:, gate_cols(GG)], w[:, gate_cols(GG)], 2.0, None,
                                        ALU.mult).then_inc(set2_ready, 1)
            nc.gpsimd.tensor_scalar(w1[:], w1[:], 1.0 / H_UNIT, None, ALU.mult).then_inc(set2_ready, 1)
            pool.wait_ge(set2_ready, SET2)
            split_wh(pool, nc.gpsimd, 1)

        OUTER_BANKS = [bankU, bankY]
        UP_BANKS = [bankU, cell, figbank[0], obank[0]]

        @block.tensor
        def _(pe):
            def gate_out(p, g):
                if g == GO:
                    return obank[p][:, 0:P]
                return figbank[p][:, 0:3 * P].rearrange("p (t g b) -> p t g b", g=3, b=NB)[:, :, FIG.index(g), :]

            def moving(tile, g):
                return tile if g == GO else tile.rearrange("p (t b) -> p t b", b=NB)

            def bias_gate(layer, p, g):
                return nc.tensor.matmul(gate_out(p, g), bias[layer][:, gate_cols(g)], moving(ones[:, :], g),
                                        start=g in (FIG[0], GO), stop=False, skip_group_check=True)

            def project_gate(layer, p, g, tile):
                return nc.tensor.matmul(gate_out(p, g), wx[layer][:, gate_cols(g)], moving(tile, g),
                                        start=False, stop=False, skip_group_check=True)

            def keep_warm(bank, n):
                for _ in range(n):
                    nc.tensor.matmul(bank[:, :], warm_w[:], warm_x[:], start=True, stop=True)

            def initial(layer):
                for g in FIG + [GO]:
                    dst = obank[0][:, 0:NB] if g == GO else figbank[0][:, FIG.index(g) * NB:FIG.index(g) * NB + NB]
                    nc.tensor.matmul(dst, wh[layer][:, gate_cols(g)], h0[:], start=False, stop=True,
                                     skip_group_check=True)

            def step(layer, s, count):
                p, t = s // CH, s % CH
                def passes(h, gs):
                    for g in gs:
                        if g == GO:
                            dst = obank[p][:, NB * t:NB * t + NB]
                        else:
                            c0 = (3 * t + FIG.index(g)) * NB
                            dst = figbank[p][:, c0:c0 + NB]
                        for part in range(3):
                            last = nc.tensor.matmul(dst, wh_parts[layer][:, part, gate_cols(g)],
                                                    h[:, (s - 1) % STEPS, :],
                                                    start=False, stop=True, skip_group_check=True)
                    return last

                pe.wait_ge(hi_ready[layer], count)
                passes(h_hi, FIG)
                pe.wait_ge(lo_ready[layer], count)
                passes(h_lo, FIG).then_inc(fig_ready[layer], 1)
                passes(h_hi, [GO])
                passes(h_lo, [GO]).then_inc(o_ready[layer], 1)

            first_two = hist[:, 0:2, :].rearrange("p c n -> p (c n)")
            pe.wait_ge(consts_ready, 1)
            keep_warm(bankV, 4)
            pe.wait_ge(consts_ready, 2)
            pe.wait_ge(ident_ready, 2)
            pe.wait_ge(rows_loaded[0], 16)
            nc.tensor.transpose(bankU[:, 0:P], x_rows[:, 0, :], ident[:]).then_inc(x_transposed, 1)
            pe.wait_ge(batch_ready, 1)
            nc.tensor.matmul(bankY[:, P:2 * P], batch_of[:], batch_of[:], start=True, stop=True)
            keep_warm(bankV, 1)
            nc.tensor.matmul(bankV[:, 0:2 * P], warm_w[:], zeros[:], start=True, stop=True, skip_group_check=True)
            pe.wait_ge(bias_ready, 1)
            for g in FIG + [GO]:
                bias_gate(0, 0, g)
            pe.wait_ge(cond_loaded, 16)
            nc.tensor.transpose(bankY[:, 0:NB], cond_rows[:], ident[0:NB, 0:NB]).then_inc(cond_transposed, 1)
            pe.wait_ge(xT_kept, 1)
            pe.wait_ge(wx_ready, 1)
            for g in FIG + [GO]:
                project_gate(0, 0, g, xT[:, 0, :])
            pe.wait_ge(h0_kept, 1)
            pe.wait_ge(wh_ready, 1)
            initial(0)
            pe.wait_ge(attn_w_loaded, 48)
            nc.tensor.matmul(bankY[:, 0:P], wtp[:, 1, :], wtp[:, 0, :], start=True, stop=True)
            nc.tensor.matmul(bankY[:, 2 * P:3 * P], wtp[:, 0, :], wtp[:, 1, :], start=True, stop=True)
            nc.tensor.transpose(bankY[:, P:2 * P], wg_rows[:], ident[:]).then_inc(proj_ready, 1)
            pe.wait_ge(parts_ready[0], 4)

            def row_products(half, bank):
                nc.tensor.matmul(bank[:, 0:2 * D], ring[:, CH * half:CH * half + CH, :].rearrange("p t b -> p (t b)"),
                                 proj[:].rearrange("p a n -> p (a n)"), start=True, stop=True).then_inc(rows_ready, 1)

            def score_products(c0, keys, q0, n):
                return nc.tensor.matmul(bankY[:, 2 * P + c0:2 * P + c0 + n], keys, queries[:, q0:q0 + n],
                                        start=True, stop=True)

            def early_attention(values, c0, q0, n):
                return nc.tensor.matmul(bankV[:, q0:q0 + n], values, scores[:, c0:c0 + n],
                                        start=False, stop=True, skip_group_check=True)

            with pe.Fori(0, ITER) as i:
                for s in range(STEPS):
                    p, t = s // CH, s % CH
                    step(0, s, i * STEPS + (s + 1))
                    if t == 0:
                        pe.wait_ge(rows_loaded[1 - p], i * 16 + 16 * (p + 1))
                        nc.tensor.transpose(bankU[:, 0:P], x_rows[:, 1 - p, :], ident[:]).then_inc(x_transposed, 1)
                        pe.wait_ge(rows_kept, i * 2 + (p + 1))
                        row_products(1 - p, bankY)
                    if t in (0, 1):
                        for g in (FIG[0:1], FIG[1:] + [GO])[t]:
                            bias_gate(0, 1 - p, g)
                    if t == 2:
                        pe.wait_ge(xT_kept, i * 2 + (p + 2))
                        nc.tensor.matmul(bankU[:, 0:2 * P], proj_at[:], first_two, start=True, stop=True
                                         ).then_inc(queries_ready, 1)
                    if t == 4:
                        pe.wait_ge(queries_kept, i * 2 + (p + 1))
                        pe.wait_ge(rows_kept, i * 2 + (p + 2))
                        score_products(0, ring[:, CH * (1 - p):CH * (2 - p), :].rearrange("p t b -> p (t b)"), 0, 2 * P
                                       ).then_inc(scores_ready, 1)
                    if t in (2, 3):
                        rhs = xT[:, bass.ds(i * 2 + (p + 1), 1), :].rearrange("p c n -> p (c n)")
                        for g in (FIG[0:1], FIG[1:] + [GO])[t - 2]:
                            project_gate(0, 1 - p, g, rhs)
                    if t == 6:
                        pe.wait_ge(scores_kept, i * 2 + (p + 1))
                        early_attention(rows[:, p, D:2 * D], 0, 0, 2 * P)
                    keep_warm(bankU, WARM1[t])

            pe.wait_ge(set2_ready, SET2)
            for g in FIG + [GO]:
                bias_gate(1, 0, g)
            last_keys = ring[:, CH:STEPS, :].rearrange("p t b -> p (t b)")
            pe.wait_ge(h_ready[0], T)
            score_products(0, last_keys, 0, P).then_inc(scores_ready, 1)
            row_products(1, bankU)
            initial(1)
            pe.wait_ge(scores_kept, NCH + 1)
            pe.wait_ge(rows_kept, NCH + 2)
            early_attention(rows[:, 0, D:2 * D], 0, 0, P).then_inc(early_attn_ready, 1)
            pe.wait_ge(x2_first, 1)
            for g in FIG + [GO]:
                last = project_gate(1, 0, g, x2T[:, 0, :])
            last.then_inc(x2_projected, 1)
            pe.wait_ge(parts_ready[1], 5)

            def outer_pair(q):
                if q >= 2:
                    pe.wait_ge(p_kept, q - 1)
                for k in range(2):
                    last = nc.tensor.matmul(OUTER_BANKS[q % len(OUTER_BANKS)][:, P * k:P * k + P],
                                            rows_t[:, 2 * q + k, 0:D], rows_t[:, 2 * q + k, D:2 * D],
                                            start=True, stop=True)
                last.then_inc(outer_ready, 1)

            hist_b = hist[:, 2:NCH, :].rearrange("p c (t b) -> p b (c t)", b=NB)
            LATE = T - STEPS

            def attend_quad(q):
                pe.wait_ge(p_kept, 2 * q + 2)
                if q >= 2:
                    pe.wait_ge(x2_done, q - 1)
                elif q == 1:
                    pe.wait_ge(p_kept, NB // 2)
                for k in range(4):
                    last = nc.tensor.matmul((bankV, bankY)[q % 2][:, LATE * k:LATE * k + LATE],
                                            p_batch[:, 4 * q + k, :],
                                            hist_b[:, 4 * q + k, :], start=True, stop=True)
                last.then_inc(late_attn_ready, 1)

            def ffn_up(half, j, bank=bankU):
                return nc.tensor.matmul(bank[:, P * j:P * j + P],
                                        w1[:, j * P:j * P + P],
                                        ring[:, CH * half:CH * half + CH, :].rearrange("p t b -> p (t b)"),
                                        start=True, stop=True)

            def ffn_down(j):
                return nc.tensor.matmul(bankY[:, 0:D], relu[:, j, :], w2[:, j, :], start=False, stop=(j == NJ - 1))

            def residual(x2):
                return nc.tensor.matmul(bankY[:, 0:D], x2, ident[:], start=True, stop=False)

            for s in range(STEPS):
                step(1, s, s + 1)
                if s == 0:
                    nc.tensor.matmul(bankU[:, 0:D], hist[:, 0, :], proj[:, 1, :], start=True, stop=True
                                     ).then_inc(rows0_ready, 1)
                    score_products(0, last_keys, P, P)
                    score_products(P, hist[:, 0, :], P, P).then_inc(scores_ready, 1)
                if s == 1:
                    for g in FIG + [GO]:
                        bias_gate(1, 1, g)
                if s == 2:
                    pe.wait_ge(scores_kept, NCH + 2)
                    pe.wait_ge(rows0_kept, 1)
                    early_attention(rows[:, 0, D:2 * D], 0, P, P)
                    early_attention(rows0[:], P, P, P).then_inc(early_attn_ready, 1)
                    keep_warm(bankU, 1)
                if s == 3:
                    pe.wait_ge(rows_moved[1], 16 * (ITER + 1))
                    pe.wait_ge(rows_moved[0], 16 * (ITER + 2))
                if s in (3, 4, 5, 6):
                    outer_pair(2 * s - 6)
                    outer_pair(2 * s - 5)
                if s == 4:
                    pe.wait_ge(x2_first, 2)
                if s in (4, 5, 6, 7):
                    last = project_gate(1, 1, (FIG + [GO])[s - 4], x2T[:, 1, :])
                if s == 7:
                    last.then_inc(x2_projected, 1)
                if s in (7, 8, 9, 10):
                    attend_quad(s - 7)
                if s in (8, 9, 10, 11):
                    bias_gate(1, 0, (FIG + [GO])[s - 8])
                if s == 11:
                    for j in range(NJ):
                        last = ffn_up(0, j)
                    last.then_inc(hidden_ready, 2)
                if s == 12:
                    pe.wait_ge(x2_done, NB // 4)
                    residual(x2T[:, 0, :])
                    for g in FIG + [GO]:
                        last = project_gate(1, 0, g, x2T[:, 2, :])
                    last.then_inc(x2_projected, 1)
                if s == 13:
                    pe.wait_ge(relu_done, 4 + 2)
                    ffn_down(0)
                    ffn_down(1)
                if s == 14:
                    pe.wait_ge(relu_done, 4 + 4)
                    ffn_down(2)
                    ffn_down(3).then_inc(y_ready, 2)
                if s >= 13:
                    keep_warm(bankV, 1 + 2 * (s == 15))
            with pe.Fori(1, ITER) as i:
                for s in range(STEPS):
                    p, t = s // CH, s % CH
                    step(1, s, i * STEPS + (s + 1))
                    c = i * 2 + p
                    if t == 0:
                        for j in range(2):
                            ffn_up(1 - p, j)
                    if t == 1:
                        for j in range(2, 4):
                            last = ffn_up(1 - p, j)
                        last.then_inc(hidden_ready, 1)
                    if t == 2:
                        pe.wait_ge(xres_loaded[1 - p], i * 16 + 16)
                        pe.wait_ge(y_copied, c + 1)
                        residual(xres[:, 1 - p, :])
                    if t == 4:
                        pe.wait_ge(relu_done, c * 4 + 2)
                        ffn_down(0)
                        ffn_down(1)
                    if t == 5:
                        pe.wait_ge(relu_done, c * 4 + 4)
                        ffn_down(2)
                        ffn_down(3).then_inc(y_ready, 1)
                    if t == 2:
                        pe.wait_ge(xin_loaded[1 - p], i * 16 + 16)
                    if t in (2, 3, 6, 7):
                        g = {2: FIG[0], 3: FIG[1], 6: FIG[2], 7: GO}[t]
                        bias_gate(1, 1 - p, g)
                        last = project_gate(1, 1 - p, g, xin[:, 1 - p, :])
                    if t == 7:
                        last.then_inc(x2_projected, 1)
                    keep_warm(bankV, WARM2[t])
            pe.wait_ge(xres_loaded[1], 16 * (ITER + 1))
            pe.wait_ge(y_copied, NCH + 1)
            residual(xres[:, 1, :])
            pe.wait_ge(h_ready[1], T)
            for j in range(NJ):
                ffn_up(1, j, UP_BANKS[j]).then_inc(hidden_ready, 1)
            for j in range(NJ):
                if j % 2 == 0:
                    pe.wait_ge(relu_done, 4 * NCH + 1 + j // 2)
                else:
                    pe.wait_ge(relu_act_done, 1 + j // 2)
                last = ffn_down(j)
            last.then_inc(y_ready, 1)

        @block.scalar
        def _(act):
            act.dma_start(wh[0][:], l1_wh).then_inc(wh1_loaded, 16)
            act.dma_start(wx[0][:], l1_wx).then_inc(wx1_loaded, 16)
            act.wait_ge(ident_ready, 2)
            nc.scalar.activation(warm[:], ident[:, 0:1], ACT.Tanh)
            act.wait_ge(x_transposed, 1)
            nc.scalar.copy(xT[:, 0, :], bankU[:, 0:P]).then_inc(xT_kept, 1)
            act.wait_ge(cond_transposed, 1)
            nc.scalar.copy(h0[:], bankY[:, 0:NB])
            nc.scalar.copy(same_batch[:].rearrange("p (c n) -> p c n", c=2),
                           bankY[:, P:2 * P].unsqueeze(1).broadcast_to([P, 2, P])).then_inc(h0_kept, 1)
            act.wait_ge(proj_ready, 1)
            nc.scalar.mul(proj[:, 0, :], bankY[:, 0:P], SC_OUT / H_UNIT ** 2)
            nc.scalar.mul(proj_at[:], bankY[:, 2 * P:3 * P], SC_OUT / H_UNIT ** 2)
            nc.scalar.mul(proj[:, 1, :], bankY[:, P:2 * P], 1.0 / H_UNIT).then_inc(rows_kept, 1)

            def step(layer, s, n):
                p, t = s // CH, s % CH
                n1 = n + 1
                act.wait_ge(fig_ready[layer], n1)
                nc.scalar.activation(gates[:, s % 2, NB:4 * NB], figbank[p][:, 3 * NB * t:3 * NB * (t + 1)],
                                     ACT.Tanh, scale=0.5).then_inc(gates_done[layer], 1)
                act.wait_ge(o_ready[layer], n1)
                nc.scalar.activation(ogate[:], obank[p][:, NB * t:NB * t + NB], ACT.Tanh,
                                     scale=0.5).then_inc(tanh_done[layer], 1)
                act.wait_ge(tanh_done[layer], n * 3 + 1)
                nc.scalar.activation(ogate1[:], ogate[:], ACT.Identity, bias=HS, scale=HS).then_inc(tanh_done[layer], 1)
                act.wait_ge(c_ready[layer], n1)
                nc.scalar.activation(tanhc, c_psum, ACT.Tanh,
                                     scale=0.5).then_inc(tanh_done[layer], 1)

            def keep_rows(slot, i, c, bank=bankY):
                act.wait_ge(rows_moved[slot], i * 16 + 16)
                act.wait_ge(rows_ready, c + 1)
                nc.scalar.copy(rows[:, slot, :], bank[:, 0:2 * D]).then_inc(rows_kept, 1)

            with act.Fori(0, ITER) as i:
                for s in range(STEPS):
                    step(0, s, i * STEPS + s)
                    p, t = s // CH, s % CH
                    if t == 1:
                        c = act.snap(i * 2 + (p + 1))
                        act.wait_ge(x_transposed, i * 2 + (p + 2))
                        nc.scalar.copy(xT[:, bass.ds(c, 1), :].rearrange("p c n -> p (c n)"),
                                       bankU[:, 0:P]).then_inc(xT_kept, 1)
                    if t == 2:
                        keep_rows(p, i, i * 2 + p)
                    if t == 3:
                        act.wait_ge(queries_ready, i * 2 + (p + 1))
                        nc.scalar.copy(queries[:], bankU[:, 0:2 * P]).then_inc(queries_kept, 1)
            keep_rows(0, ITER, NCH, bankU)
            for s in range(STEPS):
                step(1, s, s)
                if s == 0:
                    act.wait_ge(rows0_ready, 1)
                    nc.scalar.copy(rows0[:], bankU[:, 0:D]).then_inc(rows0_kept, 1)
                if s in (3, 4, 5, 6):
                    for q in (2 * s - 6, 2 * s - 5):
                        act.wait_ge(outer_ready, q + 1)
                        nc.scalar.copy(p_batch[:, 2 * q:2 * q + 2, :].rearrange("p a n -> p (a n)"),
                                       OUTER_BANKS[q % 2][:, 0:2 * D]).then_inc(p_kept, 1)
            with act.Fori(1, ITER) as i:
                for s in range(STEPS):
                    step(1, s, i * STEPS + s)
            for j in (1, 3):
                act.wait_ge(hidden_ready, NCH + 1 + j)
                nc.scalar.activation(relu[:, j, :], UP_BANKS[j][:, P * j:P * j + P], ACT.Relu,
                                     bias=b1[:, j:j + 1]).then_inc(relu_act_done, 1)

        @block.vector
        def _(dve):
            nc.vector.memset(bias[0][:], 0.0).then_inc(bias1_cleared, 1)
            nc.vector.memset(warm_w[:], 1.0)
            nc.vector.memset(warm_x[:], 1.0).then_inc(consts_ready, 1)
            nc.vector.memset(ones[:], 1.0)
            nc.vector.memset(zeros[:], 0.0).then_inc(consts_ready, 1)
            nc.vector.memset(ring[:, CH:STEPS, :], 0.0)
            nc.vector.memset(hist[:, 0:2, :], 0.0)
            dve.wait_ge(ident_ready, 2)
            nc.vector.tensor_copy(batch_of[:].rearrange("p (t b) -> p t b", b=NB),
                                  ident[0:NB, 0:NB].unsqueeze(1).broadcast_to([NB, CH, NB])).then_inc(batch_ready, 1)
            start_h(0)
            dve.wait_ge(bias1_loaded, 16)
            nc.vector.tensor_scalar(bias[0][:, gate_cols(GG)], bias[0][:, gate_cols(GG)], 2.0, None,
                                    ALU.mult).then_inc(bias_ready, 1)
            dve.wait_ge(wh1_loaded, 16)
            nc.vector.tensor_scalar(wh[0][:, gate_cols(GG)], wh[0][:, gate_cols(GG)], 2.0, None,
                                    ALU.mult).then_inc(wh_ready, 1)
            dve.wait_ge(wx1_loaded, 16)
            nc.vector.tensor_scalar(wx[0][:, gate_cols(GG)], wx[0][:, gate_cols(GG)], 2.0, None,
                                    ALU.mult).then_inc(wx_ready, 1)
            dve.wait_ge(wh_ready, 1)
            split_wh(dve, nc.vector, 0)

            def step(layer, s, n):
                p = s % 2
                n1 = n + 1
                dve.wait_ge(gates_done[layer], n1)
                nc.vector.scalar_tensor_tensor(out=prods[:], in0=gates[:, p, 2 * NB:4 * NB], scalar=1.0,
                                               in1=gates[:, p, 0:2 * NB], op0=ALU.add,
                                               op1=ALU.mult).then_inc(prod_done[layer], 1)
                dve.wait_ge(prod_done[layer], n1)
                nc.vector.scalar_tensor_tensor(out=c_psum, in0=prods[:, 0:NB], scalar=0.5,
                                               in1=prods[:, NB:2 * NB], op0=ALU.mult,
                                               op1=ALU.add).then_inc(c_ready[layer], 1)
                nc.vector.scalar_tensor_tensor(out=gates[:, 1 - p, 0:NB], in0=prods[:, 0:NB], scalar=0.5,
                                               in1=prods[:, NB:2 * NB], op0=ALU.mult,
                                               op1=ALU.add)
                dve.wait_ge(tanh_done[layer], n * 3 + 3)
                nc.vector.tensor_tensor(out=h_hi[:, s, :], in0=ogate1[:], in1=tanhc,
                                        op=ALU.mult).then_inc(hi_ready[layer], 1)
                nc.vector.tensor_tensor(out=ring[:, s, :], in0=ogate1[:], in1=tanhc,
                                        op=ALU.mult).then_inc(h_ready[layer], 1)
                dve.wait_ge(h_ready[layer], n1)
                nc.vector.tensor_tensor(out=h_lo[:, s, :], in0=ring[:, s, :], in1=h_hi[:, s, :],
                                        op=ALU.subtract).then_inc(lo_ready[layer], 1)

            def keep_scores(n):
                nc.vector.tensor_tensor(out=scores[:, 0:n], in0=bankY[:, 2 * P:2 * P + n], in1=same_batch[:, 0:n],
                                        op=ALU.mult).then_inc(scores_kept, 1)

            def early_x2(c):
                dve.wait_ge(early_attn_ready, c + 1)
                nc.vector.tensor_tensor(out=x2T[:, c, :], in0=bankV[:, P * c:P * c + P], in1=xT[:, c, :],
                                        op=ALU.add).then_inc(x2_first, 1)

            with dve.Fori(0, ITER) as i:
                for s in range(STEPS):
                    step(0, s, i * STEPS + s)
                    p, t = s // CH, s % CH
                    if t == 5:
                        dve.wait_ge(scores_ready, i * 2 + (p + 1))
                        keep_scores(2 * P)
                    if t == CH - 1:
                        c = dve.snap(i * 2 + p)
                        nc.vector.tensor_copy(hist[:, bass.ds(c, 1), :].rearrange("p c n -> p (c n)"),
                                              ring[:, CH * p:CH * p + CH, :].rearrange("p t b -> p (t b)")
                                              ).then_inc(hist_done, 1)
            dve.wait_ge(scores_ready, NCH + 1)
            keep_scores(P)
            dve.wait_ge(lo_ready[0], T + 1)
            start_h(1)
            early_x2(0)
            dve.wait_ge(set2_ready, SET2)

            def late_x2(q):
                dve.wait_ge(late_attn_ready, q + 1)
                nc.vector.tensor_tensor(out=late(x2T)[:, 4 * q:4 * q + 4],
                                        in0=(bankV, bankY)[q % 2][:, 0:4 * (T - STEPS)].rearrange(
                                            "p (b c t) -> p b c t", b=4, t=CH),
                                        in1=late(xT)[:, 4 * q:4 * q + 4], op=ALU.add).then_inc(x2_done, 1)

            def late(tile):
                return tile[:, 2:NCH, :].rearrange("p c (t b) -> p b c t", b=NB)

            dve.sem_inc(y_copied, 2)
            dve.sem_inc(relu_done, 4)

            def relu_block(j, bank=bankU):
                nc.vector.tensor_scalar(relu[:, j, :], bank[:, P * j:P * j + P],
                                        b1[:, j:j + 1], 0.0, ALU.add, ALU.max).then_inc(relu_done, 1)

            for s in range(STEPS):
                step(1, s, s)
                if s == 0:
                    dve.wait_ge(scores_ready, NCH + 2)
                    keep_scores(2 * P)
                if s == 2:
                    early_x2(1)
                if s in (7, 8, 9, 10):
                    late_x2(s - 7)
                if s == 12:
                    dve.wait_ge(hidden_ready, 2)
                    relu_block(0)
                    relu_block(1)
                if s == 13:
                    relu_block(2)
                    relu_block(3)
                if s == 15:
                    dve.wait_ge(y_stored[0], 16)
                    dve.wait_ge(y_ready, 2)
                    nc.vector.tensor_tensor(out=y_sb[:, 0, :], in0=bankY[:, 0:D], in1=b2[:],
                                            op=ALU.add).then_inc(y_copied, 1)
            with dve.Fori(1, ITER) as i:
                for s in range(STEPS):
                    p, t = s // CH, s % CH
                    step(1, s, i * STEPS + s)
                    c = i * 2 + p
                    if t == 2:
                        dve.wait_ge(hidden_ready, c + 1)
                        relu_block(0)
                        relu_block(1)
                    if t == 3:
                        relu_block(2)
                        relu_block(3)
                    if t == 6:
                        dve.wait_ge(y_stored[1 - p], i * 16 + 16)
                        dve.wait_ge(y_ready, c + 1)
                        nc.vector.tensor_tensor(out=y_sb[:, 1 - p, :], in0=bankY[:, 0:D], in1=b2[:],
                                                op=ALU.add).then_inc(y_copied, 1)
            for j in (0, 2):
                dve.wait_ge(hidden_ready, NCH + 1 + j)
                relu_block(j, UP_BANKS[j])
            dve.wait_ge(y_stored[1], 16 * ITER + 16)
            dve.wait_ge(y_ready, NCH + 1)
            nc.vector.tensor_tensor(out=y_sb[:, 1, :], in0=bankY[:, 0:D], in1=b2[:], op=ALU.add).then_inc(y_copied, 1)


_INS = ['x', 'cond_1024', 'L0_cond_Wx', 'L0_cond_Wh', 'L0_cond_b', 'L0_attn_W_theta', 'L0_attn_W_phi', 'L0_attn_W_g',
        'L0_cond2_Wx', 'L0_cond2_Wh', 'L0_cond2_b', 'L0_ffn_W1', 'L0_ffn_b1', 'L0_ffn_W2', 'L0_ffn_b2']


def kernel(**inputs):
    import numpy as _np
    import concourse.bacc as _bacc
    from concourse import mybir as _mybir
    from concourse.bass_utils import run_bass_kernel_spmd as _run

    nc = _bacc.Bacc("TRN2", target_bir_lowering=False, num_devices=1)
    arrays, args = {}, []
    for name in _INS:
        a = _np.ascontiguousarray(inputs[name])
        arrays[f"in_{name}_dram"] = a
        args.append(nc.dram_tensor(f"in_{name}_dram", a.shape, _mybir.dt.from_np(a.dtype), kind="ExternalInput").ap())
    x = inputs['x']
    out = nc.dram_tensor("out_0_dram", tuple(x.shape), _mybir.dt.float32, kind="ExternalOutput").ap()
    build(nc, *args, out)
    r = _run(nc, [arrays], core_ids=[0])
    return r.results[0]["out_0_dram"]
```
